# Optimizing a Trainium2 kernel written in Bass

```python
import numpy as np
import jax
import jax.numpy as jnp

def _softmax(x, axis=-1):
    return jax.nn.softmax(x, axis=axis)

def _gelu(x):
    return jax.nn.gelu(x, approximate=True)

def _silu(x):
    return jax.nn.silu(x)

def _sigmoid(x):
    return jax.nn.sigmoid(x)

def _layernorm(x, axis=-1, eps=1e-05):
    m = jnp.mean(x, axis=axis, keepdims=True)
    v = jnp.var(x, axis=axis, keepdims=True)
    return (x - m) / jnp.sqrt(v + eps)

def _scatter_add(tgt, idx, src, axis=0):
    return tgt.at[idx].add(src)

def _segment_sum(src, seg, n):
    return jax.ops.segment_sum(src, seg, n)
kernel_name = 'mk_macaron_d1_jaxref_r8_1f5bc4'

def setup_inputs(seed: int=0):
    np.random.seed(seed)
    _w = jnp.asarray

    def _L0_attn_setup():
        import jax, jax.numpy as jnp
        import numpy as np
        FP32_EPS = 1.1920929e-07

        def rms_norm(x):
            return x * jax.lax.rsqrt(jnp.mean(x * x, axis=-1, keepdims=True) + FP32_EPS)
        key = jax.random.key(seed)
        k1, k2, k3, k4 = jax.random.split(key, 4)
        n_embd, n_qkv = (128, 128)
        B, T = (4, 1024)

        def casted_init(k, out_f, in_f):
            s = 3.0 ** 0.5 * in_f ** (-0.5)
            return jax.random.uniform(k, (out_f, in_f), jnp.float32, -s, s)
        return {'x': jax.random.normal(k1, (B, T, n_embd), jnp.float32), 'w_qkv': casted_init(k2, 3 * n_qkv, n_embd), 'w_swiglu': casted_init(k3, 2 * n_embd, n_qkv), 'w_out': casted_init(k4, n_embd, n_embd)}
    _L0_attn_in = _L0_attn_setup()

    def _L0_ffn_setup():
        import jax, jax.numpy as jnp
        import numpy as np
        NUM_KEYS = 128
        TOP_K = 8
        NUM_HEADS = 4
        key = jax.random.key(seed)
        ks = jax.random.split(key, 8)
        b, t, d = (1, 256, 128)
        inter = 256
        E, h, ret = (2048, NUM_HEADS, 64)
        s = 0.02
        return {'hidden_states': jax.random.normal(ks[0], (b, t, d), jnp.float32), 'w_queries': jax.random.normal(ks[1], (h * ret, d), jnp.float32) * s, 'keys': jax.random.normal(ks[2], (h, NUM_KEYS, 2, ret // 2), jnp.float32) * s, 'down_embed': jax.random.normal(ks[3], (E, d), jnp.float32) * s, 'up_embed': jax.random.normal(ks[4], (E, d), jnp.float32) * s, 'w_gate': jax.random.normal(ks[5], (inter, d), jnp.float32) * s, 'w_up': jax.random.normal(ks[6], (inter, d), jnp.float32) * s, 'w_down': jax.random.normal(ks[7], (d, inter), jnp.float32) * s}
    _L0_ffn_in = _L0_ffn_setup()
    _d = {'L0_attn_x': _L0_attn_in['x'], 'L0_attn_w_qkv': _L0_attn_in['w_qkv'], 'L0_attn_w_swiglu': _L0_attn_in['w_swiglu'], 'L0_attn_w_out': _L0_attn_in['w_out'], 'L0_ffn_w_queries': _L0_ffn_in['w_queries'], 'L0_ffn_keys': _L0_ffn_in['keys'], 'L0_ffn_down_embed': _L0_ffn_in['down_embed'], 'L0_ffn_up_embed': _L0_ffn_in['up_embed'], 'L0_ffn_w_gate': _L0_ffn_in['w_gate'], 'L0_ffn_w_up': _L0_ffn_in['w_up'], 'L0_ffn_w_down': _L0_ffn_in['w_down']}
    _x0 = _d['L0_attn_x']
    _d['L0_attn_x'] = jax.random.normal(jax.random.fold_in(jax.random.key(seed), 1), (8, 1024, 128), dtype=_x0.dtype)
    del _x0
    return _d

def reference(L0_attn_x, L0_attn_w_qkv, L0_attn_w_swiglu, L0_attn_w_out, L0_ffn_w_queries, L0_ffn_keys, L0_ffn_down_embed, L0_ffn_up_embed, L0_ffn_w_gate, L0_ffn_w_up, L0_ffn_w_down):

    def _L0_attn_ref(x, w_qkv, w_swiglu, w_out):
        import jax, jax.numpy as jnp
        import numpy as np
        FP32_EPS = 1.1920929e-07

        def rms_norm(x):
            return x * jax.lax.rsqrt(jnp.mean(x * x, axis=-1, keepdims=True) + FP32_EPS)
        qkv = jnp.einsum('btd,ed->bte', rms_norm(x), w_qkv)
        q, k, v = jnp.split(qkv, 3, axis=-1)
        q = rms_norm(q)
        k = rms_norm(k)
        w = jnp.exp(k)
        kv = w * v
        w = jnp.cumsum(w, axis=1)
        kv = jnp.cumsum(kv, axis=1)
        y = kv / (w + 1e-06)
        y = jax.nn.sigmoid(q) * y
        uv = jnp.einsum('bte,fe->btf', y, w_swiglu)
        u, g = jnp.split(uv, 2, axis=-1)
        return x + jnp.einsum('btd,ed->bte', u * jax.nn.silu(g), w_out)

    def _L0_ffn_ref(hidden_states, w_queries, keys, down_embed, up_embed, w_gate, w_up, w_down):
        import jax, jax.numpy as jnp
        import numpy as np
        NUM_KEYS = 128
        TOP_K = 8
        NUM_HEADS = 4
        b, t, d = hidden_states.shape
        h, nk, _, n = keys.shape
        k = TOP_K
        q = (hidden_states @ w_queries.T).reshape(b, t, 2, h, n)
        sim = jnp.einsum('btphn,hkpn->pbthk', q, keys)
        sx, ix = jax.lax.top_k(sim[0], k)
        sy, iy = jax.lax.top_k(sim[1], k)
        all_scores = (sx[..., :, None] + sy[..., None, :]).reshape(b, t, h, k * k)
        all_idx = (ix[..., :, None] * nk + iy[..., None, :]).reshape(b, t, h, k * k)
        scores, pos = jax.lax.top_k(all_scores, k)
        indices = jnp.take_along_axis(all_idx, pos, axis=-1)
        de = down_embed[indices]
        ue = up_embed[indices]
        ew = jnp.einsum('btd,bthkd->bthk', hidden_states, de)
        ew = jax.nn.silu(ew) * jax.nn.softmax(scores, axis=-1)
        experts_states = jnp.einsum('bthk,bthkd->btd', ew, ue)
        mlp = jax.nn.silu(hidden_states @ w_gate.T) * (hidden_states @ w_up.T) @ w_down.T
        return mlp + experts_states
    x = L0_attn_x
    x = x + 0.5 * _L0_ffn_ref(_layernorm(x, axis=-1), L0_ffn_w_queries, L0_ffn_keys, L0_ffn_down_embed, L0_ffn_up_embed, L0_ffn_w_gate, L0_ffn_w_up, L0_ffn_w_down)
    x = x + _L0_attn_ref(_layernorm(x, axis=-1), L0_attn_w_qkv, L0_attn_w_swiglu, L0_attn_w_out)
    x = x + 0.5 * _L0_ffn_ref(_layernorm(x, axis=-1), L0_ffn_w_queries, L0_ffn_keys, L0_ffn_down_embed, L0_ffn_up_embed, L0_ffn_w_gate, L0_ffn_w_up, L0_ffn_w_down)
    return x

_drawn_inputs = setup_inputs


def setup_inputs(seed=0):
    import zlib

    import numpy as np

    out = dict(_drawn_inputs(seed))
    spreads = {}
    factors = {'L0_attn_w_qkv': 5.587,
     'L0_attn_w_swiglu': 3.923,
     'L0_attn_w_out': 3.924,
     'L0_ffn_w_queries': 8.0,
     'L0_ffn_keys': 23.855,
     'L0_ffn_down_embed': 8.0,
     'L0_ffn_up_embed': 8.0,
     'L0_ffn_w_gate': 8.0,
     'L0_ffn_w_up': 8.0,
     'L0_ffn_w_down': 8.0}
    for name, (base, spread) in spreads.items():
        noise = np.random.default_rng([zlib.crc32(name.encode()), seed]).standard_normal(out[name].shape)
        drawn = base * np.exp(spread * noise) if base else spread * noise
        out[name] = jnp.asarray(drawn.astype(out[name].dtype))
    for name, factor in factors.items():
        out[name] = (out[name] * factor).astype(out[name].dtype)
    return out
```

```python
from contextlib import ExitStack

import concourse.bass as bass
from concourse import mybir

F32 = mybir.dt.float32
F16 = mybir.dt.float16
U32 = mybir.dt.uint32
ALU = mybir.AluOpType
ACT = mybir.ActivationFunctionType
AX = mybir.AxisListType

P = 128
TPB = 4
H = 4
K = 8
NK = 128
NA = 16
Q = 4
GR = 32
SL = H * K
LN_EPS = 1e-5
RMS_EPS = 1.1920929e-07
CUM_EPS = 1e-6


def emit(nc, x, w_qkv_t, w_swiglu_t, w_out_t, w_queries, keys_t, down_t, up, w_gu_t, w_down_t, out):
    NT = x.shape[0] // P
    NB = NT // TPB
    x_dram = x.rearrange("(t p) d -> p t d", p=P)
    out_dram = out.rearrange("(t p) d -> p t d", p=P)

    with ExitStack() as ctx:
        def sb(name, shape, dt=F32):
            return ctx.enter_context(nc.sbuf_tensor(name, shape, dt))

        def psum(name, shape):
            return ctx.enter_context(nc.psum_tensor(name, shape, F32))

        def sem(name):
            return ctx.enter_context(nc.semaphore(name))

        x_all = sb("x_all", [P, NT, P])
        keyw = sb("keyw", [P, 2, 2 * H * NK], F16)
        down = sb("down", [P, 2, NA * P], F16)
        upw = sb("upw", [P, NA, P])
        wgu = sb("wgu", [P, 2, 512], F16)
        wdn = sb("wdn", [P, 2, P])
        w_qkv = sb("w_qkv", [P, 3 * P])
        w_sw = sb("w_sw", [P, 2 * P])
        w_o = sb("w_o", [P, P])
        iota_b = sb("iota_b", [P, P, GR], F16)
        iota_a = sb("iota_a", [P, NA, TPB * GR], F16)
        iota_k = sb("iota_k", [P, K])
        ident = sb("ident", [P, P])
        tri = sb("tri", [P, P])
        ones = sb("ones", [P, P])
        mhalf = sb("mhalf", [P, 8])
        xn = sb("xn", [P, TPB, P])
        x_t = sb("x_t", [P, TPB * P])
        xs = sb("xs", [P, 2, 2, TPB * P], F16)
        stats = sb("stats", [P, TPB, 6])
        mv = sb("mv", [P, TPB, 2])
        veps = sb("veps", [P, TPB])
        rstd = sb("rstd", [P, TPB])
        sim = sb("sim", [P, 2, 2 * H * NK])
        top = sb("top", [P, 2, TPB * H, K])
        idx = sb("idx", [P, 2, TPB * H, K], U32)
        idxf = sb("idxf", [P, 2, TPB * H, K])
        pair = sb("pair", [P, TPB * H, K, K])
        score = sb("score", [P, TPB * H, K])
        pos = sb("pos", [P, TPB * H, K], U32)
        rank = sb("rank", [P, 2, TPB * H, K], U32)
        pick = sb("pick", [P, 2, TPB * H, K, K])
        picked = sb("picked", [P, 2, TPB * H, K])
        ab = sb("ab", [P, 2, TPB * SL], F16)
        bclamp = sb("bclamp", [P, TPB * SL])
        wexp = sb("wexp", [P, TPB * H, K])
        wsum = sb("wsum", [P, TPB * H])
        a_t = sb("a_t", [P, TPB * GR], F16)
        b_t = sb("b_t", [P, 2, TPB * GR], F16)
        w_t = sb("w_t", [P, TPB * GR])
        w_hl = sb("w_hl", [P, 2, TPB * GR], F16)
        hot_a = sb("hot_a", [P, NA, TPB * GR], F16)
        vw = sb("vw", [P, 2, NA, TPB * GR], F16)
        vbd = sb("vbd", [P, 2, Q, NA, TPB * GR], F16)
        hot_b = sb("hot_b", [P, 2, P, GR], F16)
        sg = sb("sg", [P, 2, NA, P])
        act_g = sb("act_g", [P, 2, 2, TPB * P])
        act_u = sb("act_u", [P, 2, TPB * P])
        ve2 = sb("ve2", [P, 2, TPB])
        r12 = sb("r12", [P, 2, TPB])
        ssq = sb("ssq", [P, 2 * TPB])
        rqk = sb("rqk", [P, 2 * TPB])
        nrq = sb("nrq", [P, TPB])
        carrier = sb("carrier", [P, 16])
        stream = psum("stream", [P, 2, 512])
        turned = psum("turned", [P, TPB * P])
        gate = psum("gate", [P, 2, 2, 512])
        acc = psum("acc", [P, TPB, P])

        w_early = sem("w_early")
        w_late = sem("w_late")
        whi = sem("whi")
        wsplit = sem("wsplit")
        pconst = sem("pconst")
        x_in0 = sem("x_in0")
        x_in1 = sem("x_in1")
        keyw_mm = sem("keyw_mm")
        stat_d = sem("stat_d")
        rstd_d = sem("rstd_d")
        xn_d = sem("xn_d")
        xt_d = sem("xt_d")
        xcp_d = sem("xcp_d")
        xlo_d = sem("xlo_d")
        sim_mm = sem("sim_mm")
        sim_out = sem("sim_out")
        dn_mm = sem("dn_mm")
        dn_out = sem("dn_out")
        mlp_mm = sem("mlp_mm")
        mlp_out = sem("mlp_out")
        mlp_d = sem("mlp_d")
        top_d = sem("top_d")
        tail_d = sem("tail_d")
        exp_d = sem("exp_d")
        pick_d = sem("pick_d")
        v_d = sem("v_d")
        vbd_in = sem("vbd_in")
        hot_d = sem("hot_d")
        g_mm = sem("g_mm")
        sg_d = sem("sg_d")
        up_mm = sem("up_mm")
        res_d = sem("res_d")
        out_d = sem("out_d")
        mstat_d = sem("mstat_d")
        r12_d = sem("r12_d")
        xm_d = sem("xm_d")
        z_d = sem("z_d")
        xs_d = sem("xs_d")
        zt_mm = sem("zt_mm")
        zt_out = sem("zt_out")
        qkv_mm = sem("qkv_mm")
        sq_d = sem("sq_d")
        ss_d = sem("ss_d")
        rqk_d = sem("rqk_d")
        nrq_d = sem("nrq_d")
        ek_d = sem("ek_d")
        eq_d = sem("eq_d")
        kv_d = sem("kv_d")
        prior_d = sem("prior_d")
        sum_mm = sem("sum_mm")
        y_d = sem("y_d")
        yt_mm = sem("yt_mm")
        yt_out = sem("yt_out")
        uv_mm = sem("uv_mm")
        silu_d = sem("silu_d")
        h_d = sem("h_d")
        ht_mm = sem("ht_mm")
        ht_out = sem("ht_out")
        o_mm = sem("o_mm")
        mix_d = sem("mix_d")

        block = ctx.enter_context(nc.Block())

        def wait(eng, s, value):
            if isinstance(value, int) and value <= 0:
                return
            eng.wait_ge(s, value)

        carried = [0]

        def wait_apart(dve, s, value):
            wait(dve, s, value)
            carried[0] += 1
            dve.memset(carrier[:, carried[0] % 16:carried[0] % 16 + 1], 0.0)

        def schedule(eng, phase, body):
            base = phase * NB
            first = min(2, NB) if NB >= 6 else NB
            for n in range(-2, first):
                body(base, base + n, n >= 0, 0 <= n + 1 < NB, n + 2 < NB, (base + n) % 2)
            if first < NB:
                with eng.Fori(first // 2, NB // 2 - 1) as pair_no:
                    n = eng.snap(pair_no * 2 + base)
                    body(base, n, True, True, True, 0)
                    body(base, n + 1, True, True, True, 1)
                body(base, base + NB - 2, True, True, False, 0)
                body(base, base + NB - 1, True, False, False, 1)

        down_stage = sg[:, 0, :, :].rearrange("p a t -> p (a t)")
        stage = sg[:, 1, :, :].rearrange("p a t -> p (a t)")
        query_stage = stage[:, 0:2 * P].rearrange("p (s d) -> p s d", s=2)
        keys_stage = stage[:, 2 * P:4 * P].rearrange("p (s k) -> p s k", s=2)
        gu_stage = stage[:, 4 * P:8 * P]
        key_ps = [gate[:, :, :, s * NK:(s + 1) * NK].rearrange("p b c k -> p c b k") for s in range(2)]
        N_EARLY = 4
        N_SPLIT = 4
        N_CONST = 8
        STEP_SHIFTED, STEP_PICK, TAIL = 35, 38, 54

        def flat(ap):
            return ap.rearrange("p t d -> p (t d)")

        z_buf = sim[:, 0, 0:512].rearrange("p (t d) -> p t d", t=TPB)
        z_t = sim[:, 0, 512:1024]
        e_q = sim[:, 1, 0:512].rearrange("p (t d) -> p t d", t=TPB)
        y_buf = sim[:, 1, 512:1024].rearrange("p (t d) -> p t d", t=TPB)
        spare = sg[:].rearrange("p b a t -> p (b a t)")
        squares = spare[:, 0:1024]
        wkv = spare[:, 1024:2048].rearrange("p (c t d) -> p c t d", c=2, t=TPB)
        prior = spare[:, 2048:3584].rearrange("p (n c d) -> p n c d", n=6, c=2)
        y_t = spare[:, 3584:4096]
        s_gate = act_g[:, 0, 0, :].rearrange("p (t d) -> p t d", t=TPB)
        h_t = act_g[:, 0, 1, :]
        banks = gate[:].rearrange("p h c f -> p (h c) f")
        qkv = [banks[:, c, :].rearrange("p (t d) -> p t d", t=TPB) for c in range(3)]
        u_ps = banks[:, 3, :].rearrange("p (t d) -> p t d", t=TPB)
        sums = [stream[:, c, :].rearrange("p (t d) -> p t d", t=TPB) for c in range(2)]

        def attention(eng, body):
            def one(i, odd):
                body(i, i + 2 < NB, 0 <= i + 1 < NB, 0 <= i < NB, 0 <= i - 1, odd)
            first = 2 if NB >= 6 else NB + 1
            for i in range(-2, first):
                one(i, i % 2)
            if first == 2:
                with eng.Fori(1, NB // 2 - 1) as row:
                    i = eng.snap(row * 2)
                    body(i, True, True, True, True, 0)
                    body(i + 1, True, True, True, True, 1)
                for i in range(NB - 2, NB + 1):
                    one(i, i % 2)

        def attention_pe(pe):
            pe.wait_ge(res_d, NB)

            def body(i, stat, a, b, c, odd):
                if c:
                    pe.wait_ge(yt_out, i)
                    wait(pe, mix_d, i - 1)
                    for dst, w in ((u_ps, 0), (acc, 1)):
                        for t in range(TPB):
                            mm = pe.matmul(dst[:, t, :], y_t[:, t * P:(t + 1) * P], w_sw[:, w * P:(w + 1) * P],
                                           start=True, stop=True)
                    mm.then_inc(uv_mm, 1)
                if b:
                    pe.wait_ge(kv_d, i + 1)
                    wait(pe, y_d, 3 * i)
                    if odd:
                        pe.wait_ge(prior_d, 3 * i + 3)
                    for t in range(TPB):
                        tile_no = TPB * odd + t
                        if not odd and t >= 2:
                            pe.wait_ge(prior_d, 3 * i + t - 1)
                        for ch in range(2):
                            mm = pe.matmul(sums[ch][:, t, :], tri[:], wkv[:, ch, t, :], start=True, stop=tile_no == 0)
                            if tile_no:
                                before = wkv[:, ch, 0, :] if tile_no == 1 else prior[:, tile_no - 2, ch, :]
                                mm = pe.matmul(sums[ch][:, t, :], ones[:], before, start=False, stop=True)
                    mm.then_inc(sum_mm, 1)
                if a:
                    pe.wait_ge(z_d, i + 2)
                    wait(pe, yt_out, i)
                    for t in range(TPB):
                        mm = pe.transpose(turned[:, t * P:(t + 1) * P], z_buf[:, t, :], ident[:])
                    mm.then_inc(zt_mm, 1)
                    pe.wait_ge(zt_out, i + 2)
                    for ch in range(3):
                        for t in range(TPB):
                            mm = pe.matmul(qkv[ch][:, t, :], z_t[:, t * P:(t + 1) * P],
                                           w_qkv[:, ch * P:(ch + 1) * P], start=True, stop=True)
                    mm.then_inc(qkv_mm, 1)
                if c:
                    pe.wait_ge(h_d, i)
                    for t in range(TPB):
                        mm = pe.transpose(turned[:, t * P:(t + 1) * P], s_gate[:, t, :], ident[:])
                    mm.then_inc(ht_mm, 1)
                    pe.wait_ge(ht_out, i)
                    for t in range(TPB):
                        mm = pe.matmul(acc[:, t, :], h_t[:, t * P:(t + 1) * P], w_o[:], start=True, stop=True)
                    mm.then_inc(o_mm, 1)
                if b:
                    pe.wait_ge(y_d, 3 * i + 3)
                    if a:
                        pe.wait_ge(zt_out, i + 2)
                    for t in range(TPB):
                        mm = pe.transpose(turned[:, t * P:(t + 1) * P], y_buf[:, t, :], ident[:])
                    mm.then_inc(yt_mm, 1)

            attention(pe, body)

        def attention_act(act):
            def body(i, stat, a, b, c, odd):
                if b:
                    act.wait_ge(rqk_d, i + 1)
                    act.wait_ge(nrq_d, i + 1)
                    wait(act, sum_mm, i)
                    wait(act, prior_d, 3 * i)
                    for t in range(TPB):
                        act.activation(wkv[:, 0, t, :], qkv[1][:, t, :], ACT.Exp, scale=rqk[:, TPB + t:TPB + t + 1]).then_inc(ek_d, 1)
                    wait(act, y_d, 3 * i)
                    for t in range(TPB):
                        act.activation(e_q[:, t, :], qkv[0][:, t, :], ACT.Exp, scale=nrq[:, t:t + 1]).then_inc(eq_d, 1)
                    act.wait_ge(eq_d, 5 * i + 4)
                    act.activation(flat(e_q), flat(e_q), ACT.Copy, bias=1.0).then_inc(eq_d, 1)
                if c:
                    act.wait_ge(uv_mm, i)
                    wait(act, ht_mm, i - 1)
                    act.activation(flat(s_gate), flat(acc[:]), ACT.Silu).then_inc(silu_d, 1)
                if a:
                    act.wait_ge(zt_mm, i + 2)
                    act.copy(z_t, turned[:]).then_inc(zt_out, 1)
                    act.wait_ge(qkv_mm, i + 2)
                    wait(act, ss_d, 2 * (i + 1))
                    act.activation(squares, banks[:, 0:2, :].rearrange("p c f -> p (c f)"), ACT.Square).then_inc(sq_d, 1)
                if c:
                    act.wait_ge(ht_mm, i)
                    act.copy(h_t, turned[:]).then_inc(ht_out, 1)
                if b:
                    act.wait_ge(yt_mm, i + 1)
                    act.copy(y_t, turned[:]).then_inc(yt_out, 1)

            act.wait_ge(res_d, NB)
            attention(act, body)

        def attention_pool(pool):
            def body(i, stat, a, b, c, odd):
                if b:
                    pool.wait_ge(kv_d, i + 1)
                    if odd:
                        wait(pool, sum_mm, i - 1)
                        for t in range(3):
                            if t:
                                pool.wait_ge(prior_d, 3 * i + t)
                            else:
                                pool.wait_ge(prior_d, 3 * i)
                            pool.tensor_tensor(prior[:, 3 + t], prior[:, 2 + t], wkv[:, :, t, :], ALU.add).then_inc(prior_d, 1)
                    else:
                        wait(pool, sum_mm, i)
                        for t in range(3):
                            if t:
                                pool.wait_ge(prior_d, 3 * i + t)
                            pool.tensor_tensor(prior[:, t], prior[:, t - 1] if t else wkv[:, :, 0, :],
                                               wkv[:, :, t + 1, :], ALU.add).then_inc(prior_d, 1)
                if a:
                    m = i + 1
                    pool.wait_ge(xm_d, m + 1)
                    wait(pool, zt_mm, m)
                    pool.tensor_tensor(z_buf, xn[:], r12[:, 1, :, None].broadcast_to([P, TPB, P]), ALU.mult).then_inc(z_d, 1)
                    xv = x_all[:, bass.ds(m * TPB, TPB), :]
                    pool.tensor_tensor(xv, xv, xn[:], ALU.add).then_inc(xs_d, 1)
                    pool.wait_ge(ss_d, 2 * m + 2)
                    pool.tensor_tensor(rqk[:], ssq[:], mhalf[:], ALU.pow).then_inc(rqk_d, 1)
                if stat:
                    m = i + 2
                    pool.wait_ge(mstat_d, 12 * m + 12)
                    if a:
                        pool.wait_ge(z_d, i + 2)
                    pool.tensor_tensor(r12[:].rearrange("p c t -> p (c t)"), ve2[:].rearrange("p c t -> p (c t)"), mhalf[:],
                                       ALU.pow).then_inc(r12_d, 1)

            pool.wait_ge(res_d, NB)
            attention(pool, body)

        def attention_dve(dve):
            def body(i, stat, a, b, c, odd):
                if b:
                    dve.wait_ge(ek_d, 4 * i + 4)
                    dve.tensor_tensor(wkv[:, 1], wkv[:, 0], qkv[2], ALU.mult).then_inc(kv_d, 1)
                if a:
                    m = i + 1
                    dve.wait_ge(r12_d, m + 1)
                    wait(dve, xs_d, m)
                    for t in range(TPB):
                        ins = dve.tensor_scalar(xn[:, t, :], x_all[:, m * TPB + t, :], mv[:, t, 0:1],
                                                r12[:, 0, t:t + 1], ALU.subtract, ALU.mult)
                    ins.then_inc(xm_d, 1)
                if b:
                    dve.wait_ge(sum_mm, i + 1)
                    dve.wait_ge(eq_d, 5 * i + 5)
                    wait(dve, yt_mm, i)
                    dve.scalar_tensor_tensor(y_buf, sums[0], CUM_EPS, e_q, ALU.add, ALU.mult).then_inc(y_d, 1)
                    dve.wait_ge(y_d, 3 * i + 1)
                    dve.reciprocal(y_buf, y_buf).then_inc(y_d, 1)
                if c:
                    dve.wait_ge(silu_d, i)
                    dve.tensor_tensor(s_gate, s_gate, u_ps, ALU.mult).then_inc(h_d, 1)
                if b:
                    dve.wait_ge(y_d, 3 * i + 2)
                    dve.tensor_tensor(y_buf, y_buf, sums[1], ALU.mult).then_inc(y_d, 1)
                if c:
                    dve.wait_ge(o_mm, i)
                    dve.wait_ge(xs_d, i)
                    xv = x_all[:, bass.ds((i - 1) * TPB, TPB), :]
                    dve.tensor_tensor(xv, xv, acc[:], ALU.add).then_inc(mix_d, 1)
                if a:
                    m = i + 1
                    dve.wait_ge(sq_d, m + 1)
                    wait(dve, rqk_d, m)
                    dve.tensor_reduce(ssq[:], squares.rearrange("p (n d) -> p n d", d=P), AX.X, ALU.add).then_inc(ss_d, 1)
                    dve.wait_ge(ss_d, 2 * m + 1)
                    dve.tensor_scalar(ssq[:], ssq[:], 1.0 / P, RMS_EPS, ALU.mult, ALU.add).then_inc(ss_d, 1)
                if stat:
                    m = i + 2
                    wait(dve, r12_d, m)
                    for t in range(TPB):
                        dve.bn_stats(stats[:, t, :], x_all[:, m * TPB + t, :]).then_inc(mstat_d, 1)
                    wait_apart(dve, mstat_d, 12 * m + TPB)
                    for t in range(TPB):
                        dve.bn_aggr(mv[:, t, :], stats[:, t, :]).then_inc(mstat_d, 1)
                    dve.wait_ge(mstat_d, 12 * m + 8)
                    dve.tensor_scalar(ve2[:, 0, :], mv[:, :, 1], LN_EPS, None, ALU.add).then_inc(mstat_d, 1)
                    dve.wait_ge(mstat_d, 12 * m + 9)
                    dve.reciprocal(ve2[:, 1, :], ve2[:, 0, :]).then_inc(mstat_d, 1)
                    dve.wait_ge(mstat_d, 12 * m + 10)
                    dve.tensor_tensor(ve2[:, 1, :], ve2[:, 1, :], mv[:, :, 1], ALU.mult).then_inc(mstat_d, 1)
                    dve.wait_ge(mstat_d, 12 * m + 11)
                    dve.tensor_scalar(ve2[:, 1, :], ve2[:, 1, :], RMS_EPS, None, ALU.add).then_inc(mstat_d, 1)
                if a:
                    m = i + 1
                    dve.wait_ge(rqk_d, m + 1)
                    wait(dve, eq_d, 5 * m)
                    dve.tensor_scalar(nrq[:], rqk[:, 0:TPB], -1.0, None, ALU.mult).then_inc(nrq_d, 1)

            dve.wait_ge(res_d, NB)
            attention(dve, body)
            dve.wait_ge(mix_d, NB)

        @block.sync
        def _(sp):
            sp.dma_start(query_stage, w_queries.rearrange("(s r) d -> r s d", s=2)).then_inc(w_early, 16)
            sp.dma_start(keys_stage, keys_t.rearrange("s r k -> r s k")).then_inc(w_early, 16)
            nx = min(2 * TPB, NT)
            sp.dma_start(x_all[:, 0:nx, :], x_dram[:, 0:nx, :]).then_inc(x_in0, 16)
            sp.dma_start(gu_stage, w_gu_t).then_inc(w_early, 16)
            sp.dma_start(down_stage, down_t).then_inc(w_early, 16)
            sp.dma_start(upw[:], up.rearrange("(a b) d -> b a d", b=P)).then_inc(w_late, 16)
            sp.dma_start(wdn[:], w_down_t.rearrange("(c u) d -> u c d", c=2)).then_inc(w_late, 16)
            sp.dma_start(w_qkv[:], w_qkv_t).then_inc(w_late, 16)
            sp.dma_start(w_sw[:], w_swiglu_t).then_inc(w_late, 16)
            sp.dma_start(w_o[:], w_out_t).then_inc(w_late, 16)
            if NT > nx:
                sp.dma_start(x_all[:, nx:, :], x_dram[:, nx:, :]).then_inc(x_in1, 16)

            def body(base, n, cur, nxt, second, odd):
                if nxt:
                    sp.wait_ge(v_d, n + 2)
                    for q in range(Q):
                        r = slice(32 * q, 32 * q + 32)
                        sp.dma_start(vbd[r, :, q, :, :], vw[r, :, :, :]).then_inc(vbd_in, 16)
                if cur and base > 0:
                    t = (n - base) * TPB
                    sp.wait_ge(res_d, n + 1)
                    sp.dma_start(out_dram[:, bass.ds(t, TPB), :], x_all[:, bass.ds(t, TPB), :]).then_inc(out_d, 16)

            schedule(sp, 0, body)
            schedule(sp, 1, body)
            sp.wait_ge(out_d, 16 * NB)

        @block.tensor
        def _(pe):
            def prepare():
                pe.wait_ge(w_early, 16 * N_EARLY)
                for s in range(2):
                    for h in range(H):
                        r = slice(32 * h, 32 * h + 32)
                        mm = pe.matmul(gate[:, h % 2, h // 2, s * NK:(s + 1) * NK],
                                       query_stage[r, s, :], keys_stage[r, s, :], start=True, stop=True)
                mm.then_inc(keyw_mm, 1)

            def turn(n):
                pe.wait_ge(xn_d, n + 1)
                wait(pe, xcp_d, 2 * n)
                for t in range(TPB):
                    mm = pe.transpose(turned[:, t * P:(t + 1) * P], xn[:, t, :], ident[:])
                mm.then_inc(xt_d, 1)

            def sims(n, t, odd, frees):
                pe.wait_ge(xlo_d, n + 1)
                tok = slice(t * P, (t + 1) * P)
                for j in range(2):
                    wait(pe, sim_out, 8 * n + 2 * t + j - 1)
                    for s, v in frees:
                        wait(pe, s, v + j)
                    key = slice(j * 512, (j + 1) * 512)
                    pe.matmul(stream[:, j, :], xs[:, odd, 0, tok], keyw[:, 0, key], start=True, stop=False)
                    pe.matmul(stream[:, j, :], xs[:, odd, 0, tok], keyw[:, 1, key], start=False, stop=False)
                    pe.matmul(stream[:, j, :], xs[:, odd, 1, tok], keyw[:, 0, key], start=False,
                              stop=True).then_inc(sim_mm, 1)

            def experts_down(n, t, odd, frees):
                tok = slice(t * P, (t + 1) * P)
                for j in range(4):
                    wait(pe, dn_out, 16 * n + 4 * t + j - 1)
                    if j < 2:
                        for s, v in frees:
                            wait(pe, s, v + j)
                    for a in range(4 * j, 4 * j + 4):
                        o = stream[:, j % 2, (a % 4) * P:(a % 4 + 1) * P]
                        e = slice(a * P, (a + 1) * P)
                        pe.matmul(o, down[:, 0, e], xs[:, odd, 0, tok], start=True, stop=False)
                        pe.matmul(o, down[:, 0, e], xs[:, odd, 1, tok], start=False, stop=False)
                        mm = pe.matmul(o, down[:, 1, e], xs[:, odd, 0, tok], start=False, stop=True)
                    mm.then_inc(dn_mm, 1)

            def mlp_up(n, odd):
                for j in range(4):
                    if j < 2:
                        pe.wait_ge(dn_out, 16 * n + 3 + j)
                    else:
                        wait(pe, mlp_out, 4 * n + j - 1)
                    u = slice(j * P, (j + 1) * P)
                    o = stream[:, j % 2, :]
                    pe.matmul(o, wgu[:, 0, u], xs[:, odd, 0, :], start=True, stop=False)
                    pe.matmul(o, wgu[:, 0, u], xs[:, odd, 1, :], start=False, stop=False)
                    pe.matmul(o, wgu[:, 1, u], xs[:, odd, 0, :], start=False, stop=True).then_inc(mlp_mm, 1)

            def gates(n, t):
                if t == 0:
                    pe.wait_ge(vbd_in, 64 * (n + 1))
                pe.wait_ge(hot_d, 4 * n + t + 1)
                for h in range(2):
                    wait(pe, sg_d, 8 * n + 2 * t + h - 1)
                    for i in range(16):
                        g = 16 * h + i
                        o = gate[:, h, i // 8, (i % 8) * 64:(i % 8 + 1) * 64]
                        for part in range(2):
                            mm = pe.matmul(o, hot_b[:, t % 2, :, g],
                                           vbd[:, part, :, :, t * GR + g].rearrange("p q a -> p (q a)"),
                                           start=(part == 0), stop=(part == 1))
                    mm.then_inc(g_mm, 1)

            def experts_up(n, t, odd):
                if t == 0:
                    wait(pe, res_d, n)
                    pe.wait_ge(mlp_d, n + 1)
                tok = slice(t * P, (t + 1) * P)
                for c in range(2):
                    pe.matmul(acc[:, t, :], act_g[:, odd, c, tok], wdn[:, c, :], start=(c == 0), stop=False)
                pe.wait_ge(sg_d, 8 * n + 2 * t + 2)
                for a in range(NA):
                    mm = pe.matmul(acc[:, t, :], sg[:, t % 2, a, :], upw[:, a, :], start=False, stop=(a == NA - 1))
                mm.then_inc(up_mm, 1)

            def body(base, n, cur, nxt, second, odd):
                for t in range(TPB):
                    if cur:
                        gates(n, t)
                    last = t == TPB - 1
                    if last and second:
                        turn(n + 2)
                    frees = ([(mlp_out, 4 * n + 3)] if t == 0 else [(dn_out, 16 * n + 4 * t + 3)]) if cur else []
                    if second if last else nxt:
                        m, mt, modd = (n + 2, 0, odd) if last else (n + 1, t + 1, 1 - odd)
                        sims(m, mt, modd, frees)
                        frees = [(sim_out, 8 * m + 2 * mt + 1)]
                    if nxt if last else cur:
                        experts_down(*((n + 1, 0, 1 - odd) if last else (n, t + 1, odd)), frees)
                    if last and nxt:
                        mlp_up(n + 1, 1 - odd)
                    if cur:
                        experts_up(n, t, odd)

            prepare()
            pe.wait_ge(wsplit, N_SPLIT)
            pe.wait_ge(w_late, 16 * 5)
            schedule(pe, 0, body)
            attention_pe(pe)
            schedule(pe, 1, body)

        @block.scalar
        def _(act):
            def body(base, n, cur, nxt, second, odd):
                for t in range(TPB):
                    last = t == TPB - 1
                    if last and second:
                        m = n + 2
                        act.wait_ge(xt_d, m + 1)
                        act.copy(xs[:, odd, 0, :], turned[:]).then_inc(xcp_d, 1)
                        wait(act, xlo_d, m)
                        act.copy(x_t[:], turned[:]).then_inc(xcp_d, 1)
                    if second if last else nxt:
                        m, mt = (n + 2, 0) if last else (n + 1, t + 1)
                        wait(act, top_d, 16 * (4 * m + mt - 1))
                        for j in range(2):
                            act.wait_ge(sim_mm, 8 * m + 2 * mt + j + 1)
                            act.copy(sim[:, mt % 2, j * 512:(j + 1) * 512], stream[:, j, :]).then_inc(sim_out, 1)
                    if nxt if last else cur:
                        m, mt = (n + 1, 0) if last else (n, t + 1)
                        wait(act, up_mm, 4 * m + mt - 1)
                        for j in range(4):
                            act.wait_ge(dn_mm, 16 * m + 4 * mt + j + 1)
                            act.activation(sg[:, mt % 2, 4 * j:4 * j + 4, :].rearrange("p a t -> p (a t)"),
                                           stream[:, j % 2, :], ACT.Silu).then_inc(dn_out, 1)
                    if last and nxt:
                        m = n + 1
                        wait(act, up_mm, 4 * (m - 1))
                        wait(act, mlp_d, m)
                        for j in range(4):
                            act.wait_ge(mlp_mm, 4 * m + j + 1)
                            if j < 2:
                                act.activation(act_g[:, 1 - odd, j, :], stream[:, j % 2, :], ACT.Silu).then_inc(mlp_out, 1)
                            else:
                                act.copy(act_u[:, j - 2, :], stream[:, j % 2, :]).then_inc(mlp_out, 1)
                        act.wait_ge(tail_d, TAIL * m + STEP_SHIFTED)
                        act.activation(wexp[:], wexp[:], ACT.Exp).then_inc(exp_d, 1)

            act.wait_ge(w_early, 16 * N_EARLY)
            act.copy(down[:, 0, :], down_stage).then_inc(whi, 1)
            act.copy(wgu[:, 0, :], gu_stage).then_inc(whi, 1)
            act.wait_ge(keyw_mm, 1)
            act.copy(keyw[:, 0, :].rearrange("p (s h2 h1 k) -> p s h2 h1 k", s=2, h2=2, h1=2)[:, 0], key_ps[0]).then_inc(whi, 1)
            act.copy(keyw[:, 0, :].rearrange("p (s h2 h1 k) -> p s h2 h1 k", s=2, h2=2, h1=2)[:, 1], key_ps[1]).then_inc(whi, 1)
            schedule(act, 0, body)
            attention_act(act)
            schedule(act, 1, body)

        @block.gpsimd
        def _(pool):
            pool.memset(mhalf[:], -0.5).then_inc(pconst, 1)
            pool.memset(ones[:], 1.0).then_inc(pconst, 1)
            pool.iota(iota_k[:], [[1, K]], base=0, channel_multiplier=0,
                      allow_small_or_imprecise_dtypes=True).then_inc(pconst, 1)
            pool.iota(iota_b[:], [[1, P], [0, GR]], base=0, channel_multiplier=0,
                      allow_small_or_imprecise_dtypes=True).then_inc(pconst, 1)
            pool.iota(iota_a[:], [[1, NA], [0, TPB * GR]], base=0, channel_multiplier=0,
                      allow_small_or_imprecise_dtypes=True).then_inc(pconst, 1)
            pool.memset(vbd[:].rearrange("p h q a g -> p (h q a g)").bitcast(U32), 0).then_inc(pconst, 1)
            pool.wait_ge(pconst, 2)
            pool.affine_select(out=tri[:], in_=ones[:], compare_op=ALU.is_ge, fill=0.0, base=0,
                               pattern=[[1, P]], channel_multiplier=-1).then_inc(pconst, 1)
            pool.affine_select(out=ident[:], in_=ones[:], compare_op=ALU.is_equal, fill=0.0, base=0,
                               pattern=[[1, P]], channel_multiplier=-1).then_inc(pconst, 1)
            pool.wait_ge(pconst, N_CONST)

            def body(base, n, cur, nxt, second, odd):
                if second:
                    m = n + 2
                    pool.wait_ge(stat_d, 9 * m + 9)
                    pool.tensor_tensor(rstd[:], veps[:], mhalf[:, 0:TPB], ALU.pow).then_inc(rstd_d, 1)
                    pool.wait_ge(xcp_d, 2 * m + 2)
                    pool.tensor_tensor(xs[:, odd, 1, :], x_t[:], xs[:, odd, 0, :], ALU.subtract).then_inc(xlo_d, 1)
                if nxt:
                    m = n + 1
                    for s in range(2):
                        pool.wait_ge(tail_d, TAIL * m + STEP_PICK + s)
                        pool.tensor_tensor(pick[:, s], pick[:, s],
                                           idxf[:, s, :, None, :].broadcast_to([P, TPB * H, K, K]),
                                           ALU.mult).then_inc(pick_d, 1)
                    pool.wait_ge(mlp_out, 4 * m + 4)
                    g = act_g[:, 1 - odd].rearrange("p c t -> p (c t)")
                    pool.tensor_tensor(g, g, act_u[:].rearrange("p c t -> p (c t)"), ALU.mult).then_inc(mlp_d, 1)

            schedule(pool, 0, body)
            attention_pool(pool)
            schedule(pool, 1, body)

        @block.vector
        def _(dve):
            def block_of(n, base):
                return bass.ds((n - base) * TPB, TPB)

            def statistics(n, base):
                if base == 0:
                    if isinstance(n, int) and n < 2:
                        dve.wait_ge(x_in0, 16)
                    else:
                        dve.wait_ge(x_in1, 16)
                wait(dve, rstd_d, n)
                for t in range(TPB):
                    dve.bn_stats(stats[:, t, :], x_all[:, (n - base) * TPB + t, :]).then_inc(stat_d, 1)
                wait_apart(dve, stat_d, 9 * n + TPB)
                for t in range(TPB):
                    dve.bn_aggr(mv[:, t, :], stats[:, t, :]).then_inc(stat_d, 1)
                dve.wait_ge(stat_d, 9 * n + 8)
                dve.tensor_scalar(veps[:], mv[:, :, 1], LN_EPS, None, ALU.add).then_inc(stat_d, 1)

            def normalise(n, base):
                dve.wait_ge(rstd_d, n + 1)
                wait(dve, xt_d, n)
                for t in range(TPB):
                    ins = dve.tensor_scalar(xn[:, t, :], x_all[:, (n - base) * TPB + t, :], mv[:, t, 0:1],
                                            rstd[:, t:t + 1], ALU.subtract, ALU.mult)
                ins.then_inc(xn_d, 1)

            def search(n, t):
                wait_apart(dve, sim_out, 8 * n + 2 * t + 2)
                views = [(top[:, s, t * H + h, :], idx[:, s, t * H + h, :],
                          sim[:, t % 2, (s * H + h) * NK:(s * H + h + 1) * NK]) for s in range(2) for h in range(H)]
                for best, _, keys in views:
                    dve.max(best, keys).then_inc(top_d, 1)
                wait_apart(dve, top_d, 64 * n + 16 * t + 2 * H)
                for best, where, keys in views:
                    dve.max_index(where, best, keys).then_inc(top_d, 1)

            def select(n):
                step = TAIL * n
                dve.wait_ge(top_d, 64 * n + 64)
                dve.tensor_tensor(pair[:], top[:, 0, :, :, None].broadcast_to([P, TPB * H, K, K]),
                                  top[:, 1, :, None, :].broadcast_to([P, TPB * H, K, K]), ALU.add).then_inc(tail_d, 1)
                dve.tensor_copy(idxf[:].rearrange("p s m k -> p (s m k)"),
                                idx[:].rearrange("p s m k -> p (s m k)")).then_inc(tail_d, 1)
                wait_apart(dve, tail_d, step + 1)
                for m in range(TPB * H):
                    dve.max(score[:, m, :], pair[:, m].rearrange("p i j -> p (i j)")).then_inc(tail_d, 1)
                wait_apart(dve, tail_d, step + 2 + TPB * H)
                for m in range(TPB * H):
                    dve.max_index(pos[:, m, :], score[:, m, :], pair[:, m].rearrange("p i j -> p (i j)")).then_inc(tail_d, 1)
                dve.tensor_tensor(wexp[:], score[:], score[:, :, 0:1].broadcast_to([P, TPB * H, K]),
                                  ALU.subtract).then_inc(tail_d, 1)
                dve.wait_ge(tail_d, step + 34)
                dve.tensor_scalar(rank[:, 0], pos[:], 3, None, ALU.logical_shift_right).then_inc(tail_d, 1)
                dve.tensor_scalar(rank[:, 1], pos[:], K - 1, None, ALU.bitwise_and).then_inc(tail_d, 1)
                for s in range(2):
                    dve.wait_ge(tail_d, step + 36 + s)
                    dve.tensor_tensor(pick[:, s], rank[:, s, :, :, None].broadcast_to([P, TPB * H, K, K]),
                                      iota_k[:, None, None, :].broadcast_to([P, TPB * H, K, K]),
                                      ALU.is_equal).then_inc(tail_d, 1)

            def spread(n, odd):
                step = TAIL * n
                flat = "p m k -> p (m k)"
                dve.wait_ge(exp_d, n + 1)
                dve.tensor_reduce(wsum[:], wexp[:], AX.X, ALU.add).then_inc(tail_d, 1)
                dve.wait_ge(tail_d, step + 40)
                dve.reciprocal(wsum[:], wsum[:]).then_inc(tail_d, 1)
                dve.wait_ge(tail_d, step + 41)
                dve.tensor_tensor(wexp[:], wexp[:], wsum[:, :, None].broadcast_to([P, TPB * H, K]),
                                  ALU.mult).then_inc(tail_d, 1)
                dve.wait_ge(tail_d, step + 42)
                dve.transpose(w_t[:], wexp[:].rearrange(flat)).then_inc(tail_d, 1)
                dve.wait_ge(tail_d, step + 43)
                dve.tensor_copy(w_hl[:, 0, :], w_t[:]).then_inc(tail_d, 1)
                dve.wait_ge(tail_d, step + 44)
                dve.tensor_tensor(w_hl[:, 1, :], w_t[:], w_hl[:, 0, :], ALU.subtract).then_inc(tail_d, 1)
                for s in range(2):
                    dve.wait_ge(pick_d, 2 * n + 1 + s)
                    dve.tensor_reduce(picked[:, s], pick[:, s], AX.X, ALU.add).then_inc(tail_d, 1)
                dve.wait_ge(tail_d, step + 47)
                dve.tensor_scalar(ab[:, 0, :], picked[:, 0].rearrange(flat), float(NA - 1), None, ALU.min).then_inc(tail_d, 1)
                dve.tensor_scalar(bclamp[:], picked[:, 0].rearrange(flat), float(NA), float(P - 1), ALU.is_ge,
                                  ALU.mult).then_inc(tail_d, 1)
                dve.wait_ge(tail_d, step + 49)
                dve.tensor_tensor(ab[:, 1, :], bclamp[:], picked[:, 1].rearrange(flat), ALU.max).then_inc(tail_d, 1)
                dve.transpose(a_t[:], ab[:, 0, :]).then_inc(tail_d, 1)
                dve.wait_ge(tail_d, step + 51)
                dve.transpose(b_t[:, odd, :], ab[:, 1, :]).then_inc(tail_d, 1)
                dve.tensor_tensor(hot_a[:], iota_a[:], a_t[:, None, :].broadcast_to([P, NA, TPB * GR]),
                                  ALU.is_equal).then_inc(tail_d, 1)
                dve.wait_ge(tail_d, step + 53)
                wait(dve, vbd_in, 64 * n)
                for part in range(2):
                    ins = dve.tensor_tensor(vw[:, part], hot_a[:], w_hl[:, part, None, :].broadcast_to([P, NA, TPB * GR]),
                                            ALU.mult)
                    if part == 0:
                        ins.then_inc(tail_d, 1)
                ins.then_inc(v_d, 1)

            def one_hot(n, t, odd):
                wait(dve, g_mm, 8 * n + 2 * t - 2)
                dve.tensor_tensor(hot_b[:, t % 2], iota_b[:],
                                  b_t[:, odd, None, t * GR:(t + 1) * GR].broadcast_to([P, P, GR]),
                                  ALU.is_equal).then_inc(hot_d, 1)

            def weigh(n, t):
                dve.wait_ge(dn_out, 16 * n + 4 * t + 4)
                for h in range(2):
                    dve.wait_ge(g_mm, 8 * n + 2 * t + h + 1)
                    s = sg[:, t % 2].rearrange("p a (q g) -> p a q g", q=Q)[:, :, :, 16 * h:16 * h + 16]
                    g = gate[:, h].rearrange("p c f -> p (c f)").rearrange("p (g q a) -> p a q g", q=Q, a=NA)
                    dve.tensor_tensor(s, s, g, ALU.mult).then_inc(sg_d, 1)

            def residual(n, base):
                dve.wait_ge(up_mm, 4 * n + 4)
                xv = x_all[:, block_of(n, base), :]
                dve.scalar_tensor_tensor(xv, acc[:], 0.5, xv, ALU.mult, ALU.add).then_inc(res_d, 1)

            def body(base, n, cur, nxt, second, odd):
                if cur:
                    one_hot(n, 0, odd)
                for t in range(TPB):
                    if t == 2 and second:
                        statistics(n + 2, base)
                    if cur and t < TPB - 1:
                        one_hot(n, t + 1, odd)
                    if nxt:
                        search(n + 1, t)
                    if t == 0 and cur and not (isinstance(n, int) and n == base):
                        residual(n - 1, base)
                    if t == TPB - 1 and nxt:
                        select(n + 1)
                    if cur:
                        weigh(n, t)
                    if t == 2 and second:
                        normalise(n + 2, base)
                if nxt:
                    spread(n + 1, 1 - odd)
                if isinstance(n, int) and n == base + NB - 1:
                    residual(n, base)

            dve.wait_ge(whi, 4)
            dve.tensor_tensor(down[:, 1, :], down_stage, down[:, 0, :], ALU.subtract).then_inc(wsplit, 1)
            dve.tensor_tensor(wgu[:, 1, :], gu_stage, wgu[:, 0, :], ALU.subtract).then_inc(wsplit, 1)
            for s in range(2):
                v = [keyw[:, i, :].rearrange("p (s h2 h1 k) -> p s h2 h1 k", s=2, h2=2, h1=2)[:, s] for i in range(2)]
                dve.tensor_tensor(v[1], key_ps[s], v[0], ALU.subtract).then_inc(wsplit, 1)
            dve.wait_ge(pconst, N_CONST)
            schedule(dve, 0, body)
            attention_dve(dve)
            schedule(dve, 1, body)


def build_args(nc, arrays):
    names = ["x", "w_qkv_t", "w_swiglu_t", "w_out_t", "w_queries", "keys_t", "down_t", "up", "w_gu_t", "w_down_t"]
    return [nc.dram_tensor(n, arrays[n].shape, mybir.dt.from_np(arrays[n].dtype), kind="ExternalInput").ap() for n in names]


def kernel(L0_attn_x, L0_attn_w_qkv, L0_attn_w_swiglu, L0_attn_w_out, L0_ffn_w_queries, L0_ffn_keys,
           L0_ffn_down_embed, L0_ffn_up_embed, L0_ffn_w_gate, L0_ffn_w_up, L0_ffn_w_down):
    import numpy as np
    import concourse.bacc as bacc
    from concourse.bass_utils import run_bass_kernel_spmd

    c = np.ascontiguousarray
    arrays = {
        "x": c(np.asarray(L0_attn_x).reshape(-1, P)),
        "w_qkv_t": c(np.asarray(L0_attn_w_qkv).T),
        "w_swiglu_t": c(np.asarray(L0_attn_w_swiglu).T),
        "w_out_t": c(np.asarray(L0_attn_w_out).T),
        "w_queries": c(np.asarray(L0_ffn_w_queries)),
        "keys_t": c(np.asarray(L0_ffn_keys).transpose(2, 0, 3, 1).reshape(2, H * 32, NK)),
        "down_t": c(np.asarray(L0_ffn_down_embed).T),
        "up": c(np.asarray(L0_ffn_up_embed)),
        "w_gu_t": c(np.concatenate([np.asarray(L0_ffn_w_gate), np.asarray(L0_ffn_w_up)]).T),
        "w_down_t": c(np.asarray(L0_ffn_w_down).T),
    }
    nc = bacc.Bacc("TRN2", target_bir_lowering=False, num_devices=1)
    args = build_args(nc, arrays)
    out = nc.dram_tensor("out", arrays["x"].shape, F32, kind="ExternalOutput").ap()
    emit(nc, *args, out)
    r = run_bass_kernel_spmd(nc, [arrays], core_ids=[0])
    return r.results[0]["out"].reshape(np.asarray(L0_attn_x).shape)
```

```python
from contextlib import ExitStack

import concourse.bass as bass
from concourse import mybir

F32 = mybir.dt.float32
F16 = mybir.dt.float16
U32 = mybir.dt.uint32
ALU = mybir.AluOpType
ACT = mybir.ActivationFunctionType
AX = mybir.AxisListType

P = 128
TPB = 4
H = 4
K = 8
NK = 128
NA = 16
Q = 4
GR = 32
SL = H * K
NP = 2 * K + (K - 2) * 2
LN_EPS = 1e-5
RMS_EPS = 1.1920929e-07
CUM_EPS = 1e-6


def emit(nc, x, w_qkv_t, w_swiglu_t, w_out_t, w_queries, keys_t, down_t, up, w_gu_t, w_down_t, out):
    NT = x.shape[0] // P
    NB = NT // TPB
    x_dram = x.rearrange("(t p) d -> p t d", p=P)
    out_dram = out.rearrange("(t p) d -> p t d", p=P)

    with ExitStack() as ctx:
        def sb(name, shape, dt=F32):
            return ctx.enter_context(nc.sbuf_tensor(name, shape, dt))

        def psum(name, shape):
            return ctx.enter_context(nc.psum_tensor(name, shape, F32))

        def sem(name):
            return ctx.enter_context(nc.semaphore(name))

        x_all = sb("x_all", [P, NT, P])
        keyw = sb("keyw", [P, 2, 2 * H * NK], F16)
        down = sb("down", [P, 2, NA * P], F16)
        upw = sb("upw", [P, NA, P])
        wgu = sb("wgu", [P, 2, 512], F16)
        wdn = sb("wdn", [P, 2, P])
        w_qkv = sb("w_qkv", [P, 3 * P])
        w_sw = sb("w_sw", [P, 2 * P])
        w_o = sb("w_o", [P, P])
        iota_b = sb("iota_b", [P, P, GR], F16)
        iota_a = sb("iota_a", [P, NA, GR], F16)
        iota_k = sb("iota_k", [P, K])
        first_pair = sb("first_pair", [P, K])
        ident = sb("ident", [P, P])
        tri = sb("tri", [P, P])
        ones = sb("ones", [P, P])
        mhalf = sb("mhalf", [P, 8])
        xn = sb("xn", [P, TPB, P])
        x_t = sb("x_t", [P, TPB * P])
        xs = sb("xs", [P, 2, 2, TPB * P], F16)
        stats = sb("stats", [P, TPB, 6])
        mv = sb("mv", [P, TPB, 2])
        veps = sb("veps", [P, TPB])
        rstd = sb("rstd", [P, TPB])
        sim = sb("sim", [P, 2, 2 * H * NK])
        top = sb("top", [P, 2, TPB * H, K])
        idx_x = sb("idx_x", [P, TPB * H, 1 + K], U32)
        idx_y = sb("idx_y", [P, TPB * H, K], U32)
        value = sb("value", [P, 2, TPB * H, K])
        pair = sb("pair", [P, TPB * H, NP])
        score = sb("score", [P, TPB * H, K])
        pos = sb("pos", [P, TPB * H, K], U32)
        bits = sb("bits", [P, TPB * H, K], U32)
        rank_y = sb("rank_y", [P, TPB * H, K], U32)
        pick = sb("pick", [P, 2, TPB * H, K, K])
        picked = sb("picked", [P, 2, TPB * H, K])
        ab = sb("ab", [P, 2, TPB * SL], F16)
        bclamp = sb("bclamp", [P, TPB * SL])
        wexp = sb("wexp", [P, TPB * H, K])
        wsum = sb("wsum", [P, TPB * H])
        a_t = sb("a_t", [P, TPB * GR], F16)
        b_t = sb("b_t", [P, 2, TPB * GR], F16)
        w_t = sb("w_t", [P, TPB * GR])
        w_hl = sb("w_hl", [P, 2, TPB * GR], F16)
        hot_a = sb("hot_a", [P, TPB, NA, GR], F16)
        vw = sb("vw", [P, TPB, 2, NA, GR], F16)
        vbd = sb("vbd", [P, TPB, Q, 2, NA, GR], F16)
        hot_b = sb("hot_b", [P, 2, P, GR], F16)
        sg = sb("sg", [P, 2, NA, P])
        act_g = sb("act_g", [P, 2, 2, TPB * P])
        act_u = sb("act_u", [P, 2, TPB * P])
        ve2 = sb("ve2", [P, 2, TPB])
        r12 = sb("r12", [P, 2, TPB])
        ssq = sb("ssq", [P, 2 * TPB])
        rqk = sb("rqk", [P, 2 * TPB])
        nrq = sb("nrq", [P, TPB])
        carrier = sb("carrier", [P, 16])
        stream = psum("stream", [P, 2, 512])
        turned = psum("turned", [P, TPB * P])
        gate = psum("gate", [P, 2, 2, 512])
        acc = psum("acc", [P, TPB, P])

        w_early = sem("w_early")
        w_late = sem("w_late")
        whi = sem("whi")
        wsplit = sem("wsplit")
        pconst = sem("pconst")
        x_in0 = sem("x_in0")
        x_in1 = sem("x_in1")
        keyw_mm = sem("keyw_mm")
        stat_d = sem("stat_d")
        rstd_d = sem("rstd_d")
        xn_d = sem("xn_d")
        xt_d = sem("xt_d")
        xcp_d = sem("xcp_d")
        xlo_d = sem("xlo_d")
        sim_mm = sem("sim_mm")
        sim_out = sem("sim_out")
        dn_mm = sem("dn_mm")
        dn_out = sem("dn_out")
        mlp_mm = sem("mlp_mm")
        mlp_out = sem("mlp_out")
        mlp_d = sem("mlp_d")
        top_d = sem("top_d")
        tail_d = sem("tail_d")
        exp_d = sem("exp_d")
        pick_d = sem("pick_d")
        v0_d = sem("v0_d")
        v_d = sem("v_d")
        vlo_d = sem("vlo_d")
        vbd0_in = sem("vbd0_in")
        vbd_in = sem("vbd_in")
        hot_d = sem("hot_d")
        g_mm = sem("g_mm")
        sg_d = sem("sg_d")
        up_mm = sem("up_mm")
        res_d = sem("res_d")
        out_d = sem("out_d")
        mstat_d = sem("mstat_d")
        r12_d = sem("r12_d")
        xm_d = sem("xm_d")
        z_d = sem("z_d")
        xs_d = sem("xs_d")
        zt_mm = sem("zt_mm")
        zt_out = sem("zt_out")
        qkv_mm = sem("qkv_mm")
        sq_d = sem("sq_d")
        ss_d = sem("ss_d")
        rqk_d = sem("rqk_d")
        nrq_d = sem("nrq_d")
        ek_d = sem("ek_d")
        eq_d = sem("eq_d")
        kv_d = sem("kv_d")
        prior_d = sem("prior_d")
        sum_mm = sem("sum_mm")
        y_d = sem("y_d")
        yt_mm = sem("yt_mm")
        yt_out = sem("yt_out")
        uv_mm = sem("uv_mm")
        silu_d = sem("silu_d")
        h_d = sem("h_d")
        ht_mm = sem("ht_mm")
        ht_out = sem("ht_out")
        o_mm = sem("o_mm")
        mix_d = sem("mix_d")

        block = ctx.enter_context(nc.Block())

        def wait(eng, s, value):
            if isinstance(value, int) and value <= 0:
                return
            eng.wait_ge(s, value)

        carried = [0]

        def wait_apart(dve, s, value):
            wait(dve, s, value)
            carried[0] += 1
            dve.memset(carrier[:, carried[0] % 16:carried[0] % 16 + 1], 0.0)

        def schedule(eng, phase, body):
            base = phase * NB
            first = min(2, NB) if NB >= 6 else NB
            for n in range(-2, first):
                body(base, base + n, n >= 0, 0 <= n + 1 < NB, n + 2 < NB, (base + n) % 2)
            if first < NB:
                with eng.Fori(first // 2, NB // 2 - 1) as pair_no:
                    n = eng.snap(pair_no * 2 + base)
                    body(base, n, True, True, True, 0)
                    body(base, n + 1, True, True, True, 1)
                body(base, base + NB - 2, True, True, False, 0)
                body(base, base + NB - 1, True, False, False, 1)

        down_stage = sg[:, 0, :, :].rearrange("p a t -> p (a t)")
        stage = sg[:, 1, :, :].rearrange("p a t -> p (a t)")
        query_stage = stage[:, 0:2 * P].rearrange("p (s d) -> p s d", s=2)
        keys_stage = stage[:, 2 * P:4 * P].rearrange("p (s k) -> p s k", s=2)
        gu_stage = stage[:, 4 * P:8 * P]
        key_ps = [gate[:, :, :, s * NK:(s + 1) * NK].rearrange("p b c k -> p c b k") for s in range(2)]
        N_EARLY = 4
        N_SPLIT = 4
        N_CONST = 11
        steps = (["pairs_a", "pairs_b", "value_x", "value_y"] + ["score"] * (TPB * H) + ["pos"] * (TPB * H)
                 + ["shifted", "pick_x", "bits", "rank_y", "pick_y", "wsum", "winv", "weight", "w_t", "w_hi", "w_lo",
                    "picked", "a", "bclamp", "b", "a_t", "b_t", "hot_a"])
        TAIL = len(steps)

        def at(n, step):
            return TAIL * n + TAIL - steps[::-1].index(step)

        def flat(ap):
            return ap.rearrange("p t d -> p (t d)")

        z_buf = sim[:, 0, 0:512].rearrange("p (t d) -> p t d", t=TPB)
        z_t = sim[:, 0, 512:1024]
        e_q = sim[:, 1, 0:512].rearrange("p (t d) -> p t d", t=TPB)
        y_buf = sim[:, 1, 512:1024].rearrange("p (t d) -> p t d", t=TPB)
        spare = sg[:].rearrange("p b a t -> p (b a t)")
        squares = spare[:, 0:1024]
        wkv = spare[:, 1024:2048].rearrange("p (c t d) -> p c t d", c=2, t=TPB)
        prior = spare[:, 2048:3584].rearrange("p (n c d) -> p n c d", n=6, c=2)
        y_t = spare[:, 3584:4096]
        s_gate = act_g[:, 0, 0, :].rearrange("p (t d) -> p t d", t=TPB)
        h_t = act_g[:, 0, 1, :]
        banks = gate[:].rearrange("p h c f -> p (h c) f")
        qkv = [banks[:, c, :].rearrange("p (t d) -> p t d", t=TPB) for c in range(3)]
        u_ps = banks[:, 3, :].rearrange("p (t d) -> p t d", t=TPB)
        sums = [stream[:, c, :].rearrange("p (t d) -> p t d", t=TPB) for c in range(2)]

        def attention(eng, body):
            def one(i, odd):
                body(i, i + 2 < NB, 0 <= i + 1 < NB, 0 <= i < NB, 0 <= i - 1, odd)
            first = 2 if NB >= 6 else NB + 1
            for i in range(-2, first):
                one(i, i % 2)
            if first == 2:
                with eng.Fori(1, NB // 2 - 1) as row:
                    i = eng.snap(row * 2)
                    body(i, True, True, True, True, 0)
                    body(i + 1, True, True, True, True, 1)
                for i in range(NB - 2, NB + 1):
                    one(i, i % 2)

        def attention_pe(pe):
            pe.wait_ge(res_d, NB)

            def body(i, stat, a, b, c, odd):
                if c:
                    pe.wait_ge(yt_out, i)
                    wait(pe, mix_d, i - 1)
                    for dst, w in ((u_ps, 0), (acc, 1)):
                        for t in range(TPB):
                            mm = pe.matmul(dst[:, t, :], y_t[:, t * P:(t + 1) * P], w_sw[:, w * P:(w + 1) * P],
                                           start=True, stop=True)
                    mm.then_inc(uv_mm, 1)
                if b:
                    pe.wait_ge(kv_d, i + 1)
                    wait(pe, y_d, 3 * i)
                    if odd:
                        pe.wait_ge(prior_d, 3 * i + 3)
                    for t in range(TPB):
                        tile_no = TPB * odd + t
                        if not odd and t >= 2:
                            pe.wait_ge(prior_d, 3 * i + t - 1)
                        for ch in range(2):
                            mm = pe.matmul(sums[ch][:, t, :], tri[:], wkv[:, ch, t, :], start=True, stop=tile_no == 0)
                            if tile_no:
                                before = wkv[:, ch, 0, :] if tile_no == 1 else prior[:, tile_no - 2, ch, :]
                                mm = pe.matmul(sums[ch][:, t, :], ones[:], before, start=False, stop=True)
                    mm.then_inc(sum_mm, 1)
                if a:
                    pe.wait_ge(z_d, i + 2)
                    wait(pe, yt_out, i)
                    for t in range(TPB):
                        mm = pe.transpose(turned[:, t * P:(t + 1) * P], z_buf[:, t, :], ident[:])
                    mm.then_inc(zt_mm, 1)
                    pe.wait_ge(zt_out, i + 2)
                    for ch in range(3):
                        for t in range(TPB):
                            mm = pe.matmul(qkv[ch][:, t, :], z_t[:, t * P:(t + 1) * P],
                                           w_qkv[:, ch * P:(ch + 1) * P], start=True, stop=True)
                    mm.then_inc(qkv_mm, 1)
                if c:
                    pe.wait_ge(h_d, i)
                    for t in range(TPB):
                        mm = pe.transpose(turned[:, t * P:(t + 1) * P], s_gate[:, t, :], ident[:])
                    mm.then_inc(ht_mm, 1)
                    pe.wait_ge(ht_out, i)
                    for t in range(TPB):
                        mm = pe.matmul(acc[:, t, :], h_t[:, t * P:(t + 1) * P], w_o[:], start=True, stop=True)
                    mm.then_inc(o_mm, 1)
                if b:
                    pe.wait_ge(y_d, 3 * i + 3)
                    if a:
                        pe.wait_ge(zt_out, i + 2)
                    for t in range(TPB):
                        mm = pe.transpose(turned[:, t * P:(t + 1) * P], y_buf[:, t, :], ident[:])
                    mm.then_inc(yt_mm, 1)

            attention(pe, body)

        def attention_act(act):
            def body(i, stat, a, b, c, odd):
                if b:
                    act.wait_ge(rqk_d, i + 1)
                    act.wait_ge(nrq_d, i + 1)
                    wait(act, sum_mm, i)
                    wait(act, prior_d, 3 * i)
                    for t in range(TPB):
                        act.activation(wkv[:, 0, t, :], qkv[1][:, t, :], ACT.Exp, scale=rqk[:, TPB + t:TPB + t + 1]).then_inc(ek_d, 1)
                    wait(act, y_d, 3 * i)
                    for t in range(TPB):
                        act.activation(e_q[:, t, :], qkv[0][:, t, :], ACT.Exp, scale=nrq[:, t:t + 1]).then_inc(eq_d, 1)
                    act.wait_ge(eq_d, 5 * i + 4)
                    act.activation(flat(e_q), flat(e_q), ACT.Copy, bias=1.0).then_inc(eq_d, 1)
                if c:
                    act.wait_ge(uv_mm, i)
                    wait(act, ht_mm, i - 1)
                    act.activation(flat(s_gate), flat(acc[:]), ACT.Silu).then_inc(silu_d, 1)
                if a:
                    act.wait_ge(zt_mm, i + 2)
                    act.copy(z_t, turned[:]).then_inc(zt_out, 1)
                    act.wait_ge(qkv_mm, i + 2)
                    wait(act, ss_d, 2 * (i + 1))
                    act.activation(squares, banks[:, 0:2, :].rearrange("p c f -> p (c f)"), ACT.Square).then_inc(sq_d, 1)
                if c:
                    act.wait_ge(ht_mm, i)
                    act.copy(h_t, turned[:]).then_inc(ht_out, 1)
                if b:
                    act.wait_ge(yt_mm, i + 1)
                    act.copy(y_t, turned[:]).then_inc(yt_out, 1)

            act.wait_ge(res_d, NB)
            attention(act, body)

        def attention_pool(pool):
            def body(i, stat, a, b, c, odd):
                if b:
                    pool.wait_ge(kv_d, i + 1)
                    if odd:
                        wait(pool, sum_mm, i - 1)
                        for t in range(3):
                            if t:
                                pool.wait_ge(prior_d, 3 * i + t)
                            else:
                                pool.wait_ge(prior_d, 3 * i)
                            pool.tensor_tensor(prior[:, 3 + t], prior[:, 2 + t], wkv[:, :, t, :], ALU.add).then_inc(prior_d, 1)
                    else:
                        wait(pool, sum_mm, i)
                        for t in range(3):
                            if t:
                                pool.wait_ge(prior_d, 3 * i + t)
                            pool.tensor_tensor(prior[:, t], prior[:, t - 1] if t else wkv[:, :, 0, :],
                                               wkv[:, :, t + 1, :], ALU.add).then_inc(prior_d, 1)
                if a:
                    m = i + 1
                    pool.wait_ge(xm_d, m + 1)
                    wait(pool, zt_mm, m)
                    pool.tensor_tensor(z_buf, xn[:], r12[:, 1, :, None].broadcast_to([P, TPB, P]), ALU.mult).then_inc(z_d, 1)
                    xv = x_all[:, bass.ds(m * TPB, TPB), :]
                    pool.tensor_tensor(xv, xv, xn[:], ALU.add).then_inc(xs_d, 1)
                    pool.wait_ge(ss_d, 2 * m + 2)
                    pool.tensor_tensor(rqk[:], ssq[:], mhalf[:], ALU.pow).then_inc(rqk_d, 1)
                if stat:
                    m = i + 2
                    pool.wait_ge(mstat_d, 12 * m + 12)
                    if a:
                        pool.wait_ge(z_d, i + 2)
                    pool.tensor_tensor(r12[:].rearrange("p c t -> p (c t)"), ve2[:].rearrange("p c t -> p (c t)"), mhalf[:],
                                       ALU.pow).then_inc(r12_d, 1)

            pool.wait_ge(res_d, NB)
            attention(pool, body)

        def attention_dve(dve):
            def body(i, stat, a, b, c, odd):
                if b:
                    dve.wait_ge(ek_d, 4 * i + 4)
                    dve.tensor_tensor(wkv[:, 1], wkv[:, 0], qkv[2], ALU.mult).then_inc(kv_d, 1)
                if a:
                    m = i + 1
                    dve.wait_ge(r12_d, m + 1)
                    wait(dve, xs_d, m)
                    for t in range(TPB):
                        ins = dve.tensor_scalar(xn[:, t, :], x_all[:, m * TPB + t, :], mv[:, t, 0:1],
                                                r12[:, 0, t:t + 1], ALU.subtract, ALU.mult)
                    ins.then_inc(xm_d, 1)
                if b:
                    dve.wait_ge(sum_mm, i + 1)
                    dve.wait_ge(eq_d, 5 * i + 5)
                    wait(dve, yt_mm, i)
                    dve.scalar_tensor_tensor(y_buf, sums[0], CUM_EPS, e_q, ALU.add, ALU.mult).then_inc(y_d, 1)
                    dve.wait_ge(y_d, 3 * i + 1)
                    dve.reciprocal(y_buf, y_buf).then_inc(y_d, 1)
                if c:
                    dve.wait_ge(silu_d, i)
                    dve.tensor_tensor(s_gate, s_gate, u_ps, ALU.mult).then_inc(h_d, 1)
                if b:
                    dve.wait_ge(y_d, 3 * i + 2)
                    dve.tensor_tensor(y_buf, y_buf, sums[1], ALU.mult).then_inc(y_d, 1)
                if c:
                    dve.wait_ge(o_mm, i)
                    dve.wait_ge(xs_d, i)
                    xv = x_all[:, bass.ds((i - 1) * TPB, TPB), :]
                    dve.tensor_tensor(xv, xv, acc[:], ALU.add).then_inc(mix_d, 1)
                if a:
                    m = i + 1
                    dve.wait_ge(sq_d, m + 1)
                    wait(dve, rqk_d, m)
                    dve.tensor_reduce(ssq[:], squares.rearrange("p (n d) -> p n d", d=P), AX.X, ALU.add).then_inc(ss_d, 1)
                    dve.wait_ge(ss_d, 2 * m + 1)
                    dve.tensor_scalar(ssq[:], ssq[:], 1.0 / P, RMS_EPS, ALU.mult, ALU.add).then_inc(ss_d, 1)
                if stat:
                    m = i + 2
                    wait(dve, r12_d, m)
                    for t in range(TPB):
                        dve.bn_stats(stats[:, t, :], x_all[:, m * TPB + t, :]).then_inc(mstat_d, 1)
                    wait_apart(dve, mstat_d, 12 * m + TPB)
                    for t in range(TPB):
                        dve.bn_aggr(mv[:, t, :], stats[:, t, :]).then_inc(mstat_d, 1)
                    dve.wait_ge(mstat_d, 12 * m + 8)
                    dve.tensor_scalar(ve2[:, 0, :], mv[:, :, 1], LN_EPS, None, ALU.add).then_inc(mstat_d, 1)
                    dve.wait_ge(mstat_d, 12 * m + 9)
                    dve.reciprocal(ve2[:, 1, :], ve2[:, 0, :]).then_inc(mstat_d, 1)
                    dve.wait_ge(mstat_d, 12 * m + 10)
                    dve.tensor_tensor(ve2[:, 1, :], ve2[:, 1, :], mv[:, :, 1], ALU.mult).then_inc(mstat_d, 1)
                    dve.wait_ge(mstat_d, 12 * m + 11)
                    dve.tensor_scalar(ve2[:, 1, :], ve2[:, 1, :], RMS_EPS, None, ALU.add).then_inc(mstat_d, 1)
                if a:
                    m = i + 1
                    dve.wait_ge(rqk_d, m + 1)
                    wait(dve, eq_d, 5 * m)
                    dve.tensor_scalar(nrq[:], rqk[:, 0:TPB], -1.0, None, ALU.mult).then_inc(nrq_d, 1)

            dve.wait_ge(res_d, NB)
            attention(dve, body)
            dve.wait_ge(mix_d, NB)

        @block.sync
        def _(sp):
            sp.dma_start(query_stage, w_queries.rearrange("(s r) d -> r s d", s=2)).then_inc(w_early, 16)
            sp.dma_start(keys_stage, keys_t.rearrange("s r k -> r s k")).then_inc(w_early, 16)
            nx = min(2 * TPB, NT)
            sp.dma_start(x_all[:, 0:nx, :], x_dram[:, 0:nx, :]).then_inc(x_in0, 16)
            sp.dma_start(gu_stage, w_gu_t).then_inc(w_early, 16)
            sp.dma_start(down_stage, down_t).then_inc(w_early, 16)
            sp.dma_start(upw[:], up.rearrange("(a b) d -> b a d", b=P)).then_inc(w_late, 16)
            sp.dma_start(wdn[:], w_down_t.rearrange("(c u) d -> u c d", c=2)).then_inc(w_late, 16)
            sp.dma_start(w_qkv[:], w_qkv_t).then_inc(w_late, 16)
            sp.dma_start(w_sw[:], w_swiglu_t).then_inc(w_late, 16)
            sp.dma_start(w_o[:], w_out_t).then_inc(w_late, 16)
            if NT > nx:
                sp.dma_start(x_all[:, nx:, :], x_dram[:, nx:, :]).then_inc(x_in1, 16)

            def body(base, n, cur, nxt, second, odd):
                if nxt:
                    sp.wait_ge(v0_d, n + 2)
                    for q in range(Q):
                        r = slice(32 * q, 32 * q + 32)
                        sp.dma_start(vbd[r, 0, q], vw[r, 0]).then_inc(vbd0_in, 16)
                    sp.wait_ge(v_d, n + 2)
                    sp.wait_ge(vlo_d, n + 2)
                    for q in range(Q):
                        r = slice(32 * q, 32 * q + 32)
                        sp.dma_start(vbd[r, 1:TPB, q], vw[r, 1:TPB]).then_inc(vbd_in, 16)
                if cur and base > 0:
                    t = (n - base) * TPB
                    sp.wait_ge(res_d, n + 1)
                    sp.dma_start(out_dram[:, bass.ds(t, TPB), :], x_all[:, bass.ds(t, TPB), :]).then_inc(out_d, 16)

            schedule(sp, 0, body)
            schedule(sp, 1, body)
            sp.wait_ge(out_d, 16 * NB)

        @block.tensor
        def _(pe):
            def prepare():
                pe.wait_ge(w_early, 16 * N_EARLY)
                for s in range(2):
                    for h in range(H):
                        r = slice(32 * h, 32 * h + 32)
                        mm = pe.matmul(gate[:, h % 2, h // 2, s * NK:(s + 1) * NK],
                                       query_stage[r, s, :], keys_stage[r, s, :], start=True, stop=True)
                mm.then_inc(keyw_mm, 1)

            def turn(n):
                pe.wait_ge(xn_d, n + 1)
                wait(pe, xcp_d, 2 * n)
                for t in range(TPB):
                    mm = pe.transpose(turned[:, t * P:(t + 1) * P], xn[:, t, :], ident[:])
                mm.then_inc(xt_d, 1)

            def sims(n, t, odd, frees):
                pe.wait_ge(xlo_d, n + 1)
                tok = slice(t * P, (t + 1) * P)
                for j in range(2):
                    wait(pe, sim_out, 8 * n + 2 * t + j - 1)
                    for s, v in frees:
                        wait(pe, s, v + j)
                    key = slice(j * 512, (j + 1) * 512)
                    pe.matmul(stream[:, j, :], xs[:, odd, 0, tok], keyw[:, 0, key], start=True, stop=False)
                    pe.matmul(stream[:, j, :], xs[:, odd, 0, tok], keyw[:, 1, key], start=False, stop=False)
                    pe.matmul(stream[:, j, :], xs[:, odd, 1, tok], keyw[:, 0, key], start=False,
                              stop=True).then_inc(sim_mm, 1)

            def experts_down(n, t, odd, frees):
                tok = slice(t * P, (t + 1) * P)
                for j in range(4):
                    wait(pe, dn_out, 16 * n + 4 * t + j - 1)
                    if j < 2:
                        for s, v in frees:
                            wait(pe, s, v + j)
                    for a in range(4 * j, 4 * j + 4):
                        o = stream[:, j % 2, (a % 4) * P:(a % 4 + 1) * P]
                        e = slice(a * P, (a + 1) * P)
                        pe.matmul(o, down[:, 0, e], xs[:, odd, 0, tok], start=True, stop=False)
                        pe.matmul(o, down[:, 0, e], xs[:, odd, 1, tok], start=False, stop=False)
                        mm = pe.matmul(o, down[:, 1, e], xs[:, odd, 0, tok], start=False, stop=True)
                    mm.then_inc(dn_mm, 1)

            def mlp_up(n, odd):
                for j in range(4):
                    if j < 2:
                        pe.wait_ge(dn_out, 16 * n + 3 + j)
                    else:
                        wait(pe, mlp_out, 4 * n + j - 1)
                    u = slice(j * P, (j + 1) * P)
                    o = stream[:, j % 2, :]
                    pe.matmul(o, wgu[:, 0, u], xs[:, odd, 0, :], start=True, stop=False)
                    pe.matmul(o, wgu[:, 0, u], xs[:, odd, 1, :], start=False, stop=False)
                    pe.matmul(o, wgu[:, 1, u], xs[:, odd, 0, :], start=False, stop=True).then_inc(mlp_mm, 1)

            def gates(n, t):
                if t < 2:
                    pe.wait_ge(vbd_in if t else vbd0_in, 64 * (n + 1))
                pe.wait_ge(hot_d, 4 * n + t + 1)
                for h in range(2):
                    wait(pe, sg_d, 8 * n + 2 * t + h - 1)
                    for i in range(16):
                        g = 16 * h + i
                        o = gate[:, h, i // 8, (i % 8) * 64:(i % 8 + 1) * 64]
                        for part in range(2):
                            mm = pe.matmul(o, hot_b[:, t % 2, :, g],
                                           vbd[:, t, :, part, :, g],
                                           start=(part == 0), stop=(part == 1))
                    mm.then_inc(g_mm, 1)

            def experts_up(n, t, odd):
                if t == 0:
                    wait(pe, res_d, n)
                    pe.wait_ge(mlp_d, n + 1)
                tok = slice(t * P, (t + 1) * P)
                for c in range(2):
                    pe.matmul(acc[:, t, :], act_g[:, odd, c, tok], wdn[:, c, :], start=(c == 0), stop=False)
                pe.wait_ge(sg_d, 8 * n + 2 * t + 2)
                for a in range(NA):
                    mm = pe.matmul(acc[:, t, :], sg[:, t % 2, a, :], upw[:, a, :], start=False, stop=(a == NA - 1))
                mm.then_inc(up_mm, 1)

            def body(base, n, cur, nxt, second, odd):
                for t in range(TPB):
                    last = t == TPB - 1
                    if cur and t > 0:
                        gates(n, t)
                    frees = ([(mlp_out, 4 * n + 3)] if t == 0 else [(dn_out, 16 * n + 4 * t + 3)]) if cur else []
                    if t < 2 and nxt:
                        sims(n + 1, t + 2, 1 - odd, frees if t else [])
                        frees = [(sim_out, 8 * (n + 1) + 2 * (t + 2) + 1)]
                    if last and second:
                        sims(n + 2, 0, odd, frees)
                        frees = [(sim_out, 8 * (n + 2) + 1)]
                    if nxt if last else cur:
                        experts_down(*((n + 1, 0, 1 - odd) if last else (n, t + 1, odd)), frees)
                    if last and nxt:
                        mlp_up(n + 1, 1 - odd)
                    if last and second:
                        sims(n + 2, 1, odd, [(mlp_out, 4 * (n + 1) + 3)] if nxt else [])
                    if cur and t == 0:
                        gates(n, t)
                    if t == TPB - 2 and second:
                        turn(n + 2)
                    if cur:
                        experts_up(n, t, odd)

            prepare()
            pe.wait_ge(wsplit, N_SPLIT)
            pe.wait_ge(w_late, 16 * 5)
            schedule(pe, 0, body)
            attention_pe(pe)
            schedule(pe, 1, body)

        @block.scalar
        def _(act):
            def take_sims(m, t):
                wait(act, top_d, 16 * (4 * m + t - 1))
                for j in range(2):
                    act.wait_ge(sim_mm, 8 * m + 2 * t + j + 1)
                    act.copy(sim[:, t % 2, j * 512:(j + 1) * 512], stream[:, j, :]).then_inc(sim_out, 1)

            def take_down(m, t):
                wait(act, up_mm, 4 * m + t - 1)
                for j in range(4):
                    act.wait_ge(dn_mm, 16 * m + 4 * t + j + 1)
                    act.activation(sg[:, t % 2, 4 * j:4 * j + 4, :].rearrange("p a t -> p (a t)"),
                                   stream[:, j % 2, :], ACT.Silu).then_inc(dn_out, 1)

            def take_mlp(m, odd):
                wait(act, up_mm, 4 * (m - 1))
                wait(act, mlp_d, m)
                for j in range(4):
                    act.wait_ge(mlp_mm, 4 * m + j + 1)
                    if j < 2:
                        act.activation(act_g[:, odd, j, :], stream[:, j % 2, :], ACT.Silu).then_inc(mlp_out, 1)
                    else:
                        act.copy(act_u[:, j - 2, :], stream[:, j % 2, :]).then_inc(mlp_out, 1)

            def take_turned(m, odd):
                act.wait_ge(xt_d, m + 1)
                act.copy(xs[:, odd, 0, :], turned[:]).then_inc(xcp_d, 1)
                wait(act, xlo_d, m)
                act.copy(x_t[:], turned[:]).then_inc(xcp_d, 1)

            def body(base, n, cur, nxt, second, odd):
                for t in range(TPB):
                    if t < 2 and nxt:
                        take_sims(n + 1, t + 2)
                    if t < TPB - 1:
                        if cur:
                            take_down(n, t + 1)
                        if t == TPB - 2 and second:
                            take_turned(n + 2, odd)
                        continue
                    if second:
                        take_sims(n + 2, 0)
                    if nxt:
                        take_down(n + 1, 0)
                        take_mlp(n + 1, 1 - odd)
                    if nxt:
                        act.wait_ge(tail_d, at(n + 1, "shifted"))
                        act.activation(wexp[:], wexp[:], ACT.Exp).then_inc(exp_d, 1)
                    if second:
                        take_sims(n + 2, 1)

            act.wait_ge(w_early, 16 * N_EARLY)
            act.copy(down[:, 0, :], down_stage).then_inc(whi, 1)
            act.copy(wgu[:, 0, :], gu_stage).then_inc(whi, 1)
            act.wait_ge(keyw_mm, 1)
            act.copy(keyw[:, 0, :].rearrange("p (s h2 h1 k) -> p s h2 h1 k", s=2, h2=2, h1=2)[:, 0], key_ps[0]).then_inc(whi, 1)
            act.copy(keyw[:, 0, :].rearrange("p (s h2 h1 k) -> p s h2 h1 k", s=2, h2=2, h1=2)[:, 1], key_ps[1]).then_inc(whi, 1)
            schedule(act, 0, body)
            attention_act(act)
            schedule(act, 1, body)

        @block.gpsimd
        def _(pool):
            pool.memset(mhalf[:], -0.5).then_inc(pconst, 1)
            pool.memset(ones[:], 1.0).then_inc(pconst, 1)
            pool.iota(iota_k[:], [[1, K]], base=0, channel_multiplier=0,
                      allow_small_or_imprecise_dtypes=True).then_inc(pconst, 1)
            pool.iota(iota_b[:], [[1, P], [0, GR]], base=0, channel_multiplier=0,
                      allow_small_or_imprecise_dtypes=True).then_inc(pconst, 1)
            pool.iota(iota_a[:], [[1, NA], [0, GR]], base=0, channel_multiplier=0,
                      allow_small_or_imprecise_dtypes=True).then_inc(pconst, 1)
            pool.iota(first_pair[:, 0:2], [[K, 2]], base=0, channel_multiplier=0,
                      allow_small_or_imprecise_dtypes=True).then_inc(pconst, 1)
            pool.iota(first_pair[:, 2:K], [[2, K - 2]], base=2 * K, channel_multiplier=0,
                      allow_small_or_imprecise_dtypes=True).then_inc(pconst, 1)
            pool.memset(idx_x[:, :, 0], 0).then_inc(pconst, 1)
            pool.memset(vbd[:].rearrange("p t q h a g -> p (t q h a g)").bitcast(U32), 0).then_inc(pconst, 1)
            pool.wait_ge(pconst, 2)
            pool.affine_select(out=tri[:], in_=ones[:], compare_op=ALU.is_ge, fill=0.0, base=0,
                               pattern=[[1, P]], channel_multiplier=-1).then_inc(pconst, 1)
            pool.affine_select(out=ident[:], in_=ones[:], compare_op=ALU.is_equal, fill=0.0, base=0,
                               pattern=[[1, P]], channel_multiplier=-1).then_inc(pconst, 1)
            pool.wait_ge(pconst, N_CONST)

            def body(base, n, cur, nxt, second, odd):
                if second:
                    m = n + 2
                    pool.wait_ge(stat_d, 9 * m + 9)
                    pool.tensor_tensor(rstd[:], veps[:], mhalf[:, 0:TPB], ALU.pow).then_inc(rstd_d, 1)
                    pool.wait_ge(xcp_d, 2 * m + 2)
                    pool.tensor_tensor(xs[:, odd, 1, :], x_t[:], xs[:, odd, 0, :], ALU.subtract).then_inc(xlo_d, 1)
                if nxt:
                    m = n + 1
                    for s, step in enumerate(("pick_x", "pick_y")):
                        pool.wait_ge(tail_d, at(m, step))
                        pool.tensor_tensor(pick[:, s], pick[:, s],
                                           value[:, s, :, None, :].broadcast_to([P, TPB * H, K, K]),
                                           ALU.mult).then_inc(pick_d, 1)
                    pool.wait_ge(pick_d, 3 * m + 2)
                    halves = pick[:].rearrange("p s m k i -> p (s m k) i")
                    pool.tensor_tensor(halves[:, :, 0:K // 2], halves[:, :, 0:K // 2], halves[:, :, K // 2:K],
                                       ALU.add).then_inc(pick_d, 1)
                    pool.wait_ge(mlp_out, 4 * m + 4)
                    g = act_g[:, 1 - odd].rearrange("p c t -> p (c t)")
                    pool.tensor_tensor(g, g, act_u[:].rearrange("p c t -> p (c t)"), ALU.mult).then_inc(mlp_d, 1)
                    pool.wait_ge(tail_d, at(m, "hot_a"))
                    wait(pool, vbd_in, 64 * m)
                    for t in range(1, TPB):
                        ins = pool.tensor_tensor(vw[:, t, 1], hot_a[:, t],
                                                 w_hl[:, 1, None, t * GR:(t + 1) * GR].broadcast_to([P, NA, GR]), ALU.mult)
                    ins.then_inc(vlo_d, 1)

            schedule(pool, 0, body)
            attention_pool(pool)
            schedule(pool, 1, body)

        @block.vector
        def _(dve):
            def block_of(n, base):
                return bass.ds((n - base) * TPB, TPB)

            def statistics(n, base):
                if base == 0:
                    if isinstance(n, int) and n < 2:
                        dve.wait_ge(x_in0, 16)
                    else:
                        dve.wait_ge(x_in1, 16)
                wait(dve, rstd_d, n)
                for t in range(TPB):
                    dve.bn_stats(stats[:, t, :], x_all[:, (n - base) * TPB + t, :]).then_inc(stat_d, 1)
                wait_apart(dve, stat_d, 9 * n + TPB)
                for t in range(TPB):
                    dve.bn_aggr(mv[:, t, :], stats[:, t, :]).then_inc(stat_d, 1)
                dve.wait_ge(stat_d, 9 * n + 8)
                dve.tensor_scalar(veps[:], mv[:, :, 1], LN_EPS, None, ALU.add).then_inc(stat_d, 1)

            def normalise(n, base):
                dve.wait_ge(rstd_d, n + 1)
                wait(dve, xt_d, n)
                for t in range(TPB):
                    ins = dve.tensor_scalar(xn[:, t, :], x_all[:, (n - base) * TPB + t, :], mv[:, t, 0:1],
                                            rstd[:, t:t + 1], ALU.subtract, ALU.mult)
                ins.then_inc(xn_d, 1)

            def search(n, t):
                wait_apart(dve, sim_out, 8 * n + 2 * t + 2)
                views = [(top[:, s, t * H + h, :], idx_y[:, t * H + h, :] if s else idx_x[:, t * H + h, 1:1 + K],
                          sim[:, t % 2, (s * H + h) * NK:(s * H + h + 1) * NK]) for s in range(2) for h in range(H)]
                for best, _, keys in views:
                    dve.max(best, keys).then_inc(top_d, 1)
                wait_apart(dve, top_d, 64 * n + 16 * t + 2 * H)
                for best, where, keys in views:
                    dve.max_index(where, best, keys).then_inc(top_d, 1)

            def select(n):
                every = [P, TPB * H, K, K]
                dve.wait_ge(top_d, 64 * n + 64)
                x, y = top[:, 0], top[:, 1]
                dve.tensor_tensor(pair[:, :, 0:2 * K].rearrange("p m (i j) -> p m i j", i=2),
                                  x[:, :, 0:2, None].broadcast_to([P, TPB * H, 2, K]),
                                  y[:, :, None, :].broadcast_to([P, TPB * H, 2, K]), ALU.add).then_inc(tail_d, 1)
                dve.tensor_tensor(pair[:, :, 2 * K:NP].rearrange("p m (i j) -> p m i j", j=2),
                                  x[:, :, 2:K, None].broadcast_to([P, TPB * H, K - 2, 2]),
                                  y[:, :, None, 0:2].broadcast_to([P, TPB * H, K - 2, 2]), ALU.add).then_inc(tail_d, 1)
                dve.tensor_tensor(value[:, 0], idx_x[:, :, 1:1 + K], idx_x[:, :, 0:K], ALU.subtract).then_inc(tail_d, 1)
                dve.tensor_copy(value[:, 1], idx_y[:]).then_inc(tail_d, 1)
                wait_apart(dve, tail_d, at(n, "pairs_b"))
                for m in range(TPB * H):
                    dve.max(score[:, m, :], pair[:, m, :]).then_inc(tail_d, 1)
                wait_apart(dve, tail_d, at(n, "score"))
                for m in range(TPB * H):
                    dve.max_index(pos[:, m, :], score[:, m, :], pair[:, m, :]).then_inc(tail_d, 1)
                dve.tensor_tensor(wexp[:], score[:], score[:, :, 0:1].broadcast_to([P, TPB * H, K]),
                                  ALU.subtract).then_inc(tail_d, 1)
                dve.wait_ge(tail_d, at(n, "pos"))
                dve.tensor_tensor(pick[:, 0], pos[:, :, :, None].broadcast_to(every),
                                  first_pair[:, None, None, :].broadcast_to(every), ALU.is_ge).then_inc(tail_d, 1)
                dve.tensor_scalar(bits[:], pos[:], float(2 * K), 6.0, ALU.is_lt, ALU.mult).then_inc(tail_d, 1)
                dve.wait_ge(tail_d, at(n, "bits"))
                dve.scalar_tensor_tensor(rank_y[:], bits[:], 1, pos[:], ALU.bitwise_or, ALU.bitwise_and).then_inc(tail_d, 1)
                dve.wait_ge(tail_d, at(n, "rank_y"))
                dve.tensor_tensor(pick[:, 1], rank_y[:, :, :, None].broadcast_to(every),
                                  iota_k[:, None, None, :].broadcast_to(every), ALU.is_equal).then_inc(tail_d, 1)

            def spread(n, odd):
                flat = "p m k -> p (m k)"
                dve.wait_ge(exp_d, n + 1)
                dve.tensor_reduce(wsum[:], wexp[:], AX.X, ALU.add).then_inc(tail_d, 1)
                dve.wait_ge(tail_d, at(n, "wsum"))
                dve.reciprocal(wsum[:], wsum[:]).then_inc(tail_d, 1)
                dve.wait_ge(tail_d, at(n, "winv"))
                dve.tensor_tensor(wexp[:], wexp[:], wsum[:, :, None].broadcast_to([P, TPB * H, K]),
                                  ALU.mult).then_inc(tail_d, 1)
                dve.wait_ge(tail_d, at(n, "weight"))
                dve.transpose(w_t[:], wexp[:].rearrange(flat)).then_inc(tail_d, 1)
                dve.wait_ge(tail_d, at(n, "w_t"))
                dve.tensor_copy(w_hl[:, 0, :], w_t[:]).then_inc(tail_d, 1)
                dve.wait_ge(tail_d, at(n, "w_hi"))
                dve.tensor_tensor(w_hl[:, 1, :], w_t[:], w_hl[:, 0, :], ALU.subtract).then_inc(tail_d, 1)
                dve.wait_ge(pick_d, 3 * n + 3)
                dve.tensor_reduce(picked[:], pick[:, :, :, :, 0:K // 2].rearrange("p s m k i -> p (s m k) i"), AX.X,
                                  ALU.add).then_inc(tail_d, 1)
                dve.wait_ge(tail_d, at(n, "picked"))
                dve.tensor_scalar(ab[:, 0, :], picked[:, 0].rearrange(flat), float(NA - 1), None, ALU.min).then_inc(tail_d, 1)
                dve.tensor_scalar(bclamp[:], picked[:, 0].rearrange(flat), float(NA), float(P - 1), ALU.is_ge,
                                  ALU.mult).then_inc(tail_d, 1)
                dve.wait_ge(tail_d, at(n, "bclamp"))
                dve.tensor_tensor(ab[:, 1, :], bclamp[:], picked[:, 1].rearrange(flat), ALU.max).then_inc(tail_d, 1)
                dve.transpose(a_t[:], ab[:, 0, :]).then_inc(tail_d, 1)
                dve.wait_ge(tail_d, at(n, "a_t"))
                dve.transpose(b_t[:, odd, :], ab[:, 1, :]).then_inc(tail_d, 1)
                wait(dve, vlo_d, n)
                for t in range(TPB):
                    ins = dve.tensor_tensor(hot_a[:, t], iota_a[:],
                                            a_t[:, None, t * GR:(t + 1) * GR].broadcast_to([P, NA, GR]), ALU.is_equal)
                ins.then_inc(tail_d, 1)
                dve.wait_ge(tail_d, at(n, "hot_a"))
                wait(dve, vbd0_in, 64 * n)
                for part in range(2):
                    ins = dve.tensor_tensor(vw[:, 0, part], hot_a[:, 0], w_hl[:, part, None, 0:GR].broadcast_to([P, NA, GR]),
                                            ALU.mult)
                ins.then_inc(v0_d, 1)
                wait(dve, vbd_in, 64 * n)
                for t in range(1, TPB):
                    ins = dve.tensor_tensor(vw[:, t, 0], hot_a[:, t],
                                            w_hl[:, 0, None, t * GR:(t + 1) * GR].broadcast_to([P, NA, GR]), ALU.mult)
                ins.then_inc(v_d, 1)

            def one_hot(n, t, odd):
                wait(dve, g_mm, 8 * n + 2 * t - 2)
                dve.tensor_tensor(hot_b[:, t % 2], iota_b[:],
                                  b_t[:, odd, None, t * GR:(t + 1) * GR].broadcast_to([P, P, GR]),
                                  ALU.is_equal).then_inc(hot_d, 1)

            def weigh(n, t):
                dve.wait_ge(dn_out, 16 * n + 4 * t + 4)
                for h in range(2):
                    dve.wait_ge(g_mm, 8 * n + 2 * t + h + 1)
                    s = sg[:, t % 2].rearrange("p a (q g) -> p a q g", q=Q)[:, :, :, 16 * h:16 * h + 16]
                    g = gate[:, h].rearrange("p c f -> p (c f)").rearrange("p (g q a) -> p a q g", q=Q, a=NA)
                    dve.tensor_tensor(s, s, g, ALU.mult).then_inc(sg_d, 1)

            def residual(n, base):
                dve.wait_ge(up_mm, 4 * n + 4)
                xv = x_all[:, block_of(n, base), :]
                dve.scalar_tensor_tensor(xv, acc[:], 0.5, xv, ALU.mult, ALU.add).then_inc(res_d, 1)

            def body(base, n, cur, nxt, second, odd):
                for t in range(TPB):
                    if cur and t < TPB - 1:
                        one_hot(n, t + 1, odd)
                    if t == 0 and cur and not (isinstance(n, int) and n == base):
                        residual(n - 1, base)
                    if t == 1 and second:
                        statistics(n + 2, base)
                    if t == TPB - 1 and nxt:
                        select(n + 1)
                    if cur:
                        weigh(n, t)
                    if nxt and t < TPB - 1:
                        search(n + 1, t + 1)
                    if t == 1 and second:
                        normalise(n + 2, base)
                if second:
                    search(n + 2, 0)
                if nxt:
                    spread(n + 1, 1 - odd)
                    one_hot(n + 1, 0, 1 - odd)
                if isinstance(n, int) and n == base + NB - 1:
                    residual(n, base)

            dve.wait_ge(whi, 4)
            dve.tensor_tensor(down[:, 1, :], down_stage, down[:, 0, :], ALU.subtract).then_inc(wsplit, 1)
            dve.tensor_tensor(wgu[:, 1, :], gu_stage, wgu[:, 0, :], ALU.subtract).then_inc(wsplit, 1)
            for s in range(2):
                v = [keyw[:, i, :].rearrange("p (s h2 h1 k) -> p s h2 h1 k", s=2, h2=2, h1=2)[:, s] for i in range(2)]
                dve.tensor_tensor(v[1], key_ps[s], v[0], ALU.subtract).then_inc(wsplit, 1)
            dve.wait_ge(pconst, N_CONST)
            schedule(dve, 0, body)
            attention_dve(dve)
            schedule(dve, 1, body)


def build_args(nc, arrays):
    names = ["x", "w_qkv_t", "w_swiglu_t", "w_out_t", "w_queries", "keys_t", "down_t", "up", "w_gu_t", "w_down_t"]
    return [nc.dram_tensor(n, arrays[n].shape, mybir.dt.from_np(arrays[n].dtype), kind="ExternalInput").ap() for n in names]


def kernel(L0_attn_x, L0_attn_w_qkv, L0_attn_w_swiglu, L0_attn_w_out, L0_ffn_w_queries, L0_ffn_keys,
           L0_ffn_down_embed, L0_ffn_up_embed, L0_ffn_w_gate, L0_ffn_w_up, L0_ffn_w_down):
    import numpy as np
    import concourse.bacc as bacc
    from concourse.bass_utils import run_bass_kernel_spmd

    c = np.ascontiguousarray
    arrays = {
        "x": c(np.asarray(L0_attn_x).reshape(-1, P)),
        "w_qkv_t": c(np.asarray(L0_attn_w_qkv).T),
        "w_swiglu_t": c(np.asarray(L0_attn_w_swiglu).T),
        "w_out_t": c(np.asarray(L0_attn_w_out).T),
        "w_queries": c(np.asarray(L0_ffn_w_queries)),
        "keys_t": c(np.asarray(L0_ffn_keys).transpose(2, 0, 3, 1).reshape(2, H * 32, NK)),
        "down_t": c(np.asarray(L0_ffn_down_embed).T),
        "up": c(np.asarray(L0_ffn_up_embed)),
        "w_gu_t": c(np.concatenate([np.asarray(L0_ffn_w_gate), np.asarray(L0_ffn_w_up)]).T),
        "w_down_t": c(np.asarray(L0_ffn_w_down).T),
    }
    nc = bacc.Bacc("TRN2", target_bir_lowering=False, num_devices=1)
    args = build_args(nc, arrays)
    out = nc.dram_tensor("out", arrays["x"].shape, F32, kind="ExternalOutput").ap()
    emit(nc, *args, out)
    r = run_bass_kernel_spmd(nc, [arrays], core_ids=[0])
    return r.results[0]["out"].reshape(np.asarray(L0_attn_x).shape)
```

```python
from contextlib import ExitStack

import concourse.bass as bass
from concourse import mybir

F32 = mybir.dt.float32
F16 = mybir.dt.float16
U32 = mybir.dt.uint32
ALU = mybir.AluOpType
ACT = mybir.ActivationFunctionType
AX = mybir.AxisListType

P = 128
TPB = 4
H = 4
K = 8
NK = 128
NA = 16
Q = 4
GR = 32
SL = H * K
NP = 2 * K + (K - 2) * 2
LN_EPS = 1e-5
RMS_EPS = 1.1920929e-07
CUM_EPS = 1e-6


def emit(nc, x, w_qkv_t, w_swiglu_t, w_out_t, w_queries, keys_t, down_t, up, w_gu_t, w_down_t, out):
    NT = x.shape[0] // P
    NB = NT // TPB
    x_dram = x.rearrange("(t p) d -> p t d", p=P)
    out_dram = out.rearrange("(t p) d -> p t d", p=P)

    with ExitStack() as ctx:
        def sb(name, shape, dt=F32):
            return ctx.enter_context(nc.sbuf_tensor(name, shape, dt))

        def psum(name, shape):
            return ctx.enter_context(nc.psum_tensor(name, shape, F32))

        def sem(name):
            return ctx.enter_context(nc.semaphore(name))

        x_all = sb("x_all", [P, NT, P])
        keyw = sb("keyw", [P, 2, 2 * H * NK], F16)
        down = sb("down", [P, 2, NA * P], F16)
        upw = sb("upw", [P, NA, P])
        wgu = sb("wgu", [P, 2, 512], F16)
        wdn = sb("wdn", [P, 2, P])
        w_qkv = sb("w_qkv", [P, 3 * P])
        w_sw = sb("w_sw", [P, 2 * P])
        w_o = sb("w_o", [P, P])
        iota_b = sb("iota_b", [P, P, GR], F16)
        iota_a = sb("iota_a", [P, NA, GR], F16)
        iota_k = sb("iota_k", [P, K])
        first_pair = sb("first_pair", [P, K])
        ident = sb("ident", [P, P])
        tri = sb("tri", [P, P])
        ones = sb("ones", [P, P])
        mhalf = sb("mhalf", [P, 8])
        minus = sb("minus", [P, TPB])
        xn = sb("xn", [P, TPB, P])
        x_t = sb("x_t", [P, TPB * P])
        xs = sb("xs", [P, 2, 2, TPB * P], F16)
        stats = sb("stats", [P, TPB, 6])
        mv = sb("mv", [P, TPB, 2])
        veps = sb("veps", [P, TPB])
        rstd = sb("rstd", [P, TPB])
        sim = sb("sim", [P, 2, 2 * H * NK])
        top = sb("top", [P, 2, TPB * H, K])
        idx_x = sb("idx_x", [P, TPB * H, 1 + K], U32)
        idx_y = sb("idx_y", [P, TPB * H, K], U32)
        value = sb("value", [P, 2, TPB * H, K])
        pair = sb("pair", [P, TPB * H, NP])
        score = sb("score", [P, TPB * H, K])
        pos = sb("pos", [P, TPB * H, K], U32)
        bits = sb("bits", [P, TPB * H, K], U32)
        rank_y = sb("rank_y", [P, TPB * H, K], U32)
        pick = sb("pick", [P, 2, TPB * H, K, K])
        picked = sb("picked", [P, 2, TPB * H, K])
        ab = sb("ab", [P, 2, TPB * SL], F16)
        bclamp = sb("bclamp", [P, TPB * SL])
        wexp = sb("wexp", [P, TPB * H, K])
        wsum = sb("wsum", [P, TPB * H])
        a_t = sb("a_t", [P, TPB * GR], F16)
        b_t = sb("b_t", [P, 2, TPB * GR], F16)
        w_t = sb("w_t", [P, TPB * GR])
        w_hl = sb("w_hl", [P, 2, TPB * GR], F16)
        hot_a = sb("hot_a", [P, TPB, NA, GR], F16)
        vw = sb("vw", [P, TPB, 2, NA, GR], F16)
        vbd = sb("vbd", [P, TPB, Q, 2, NA, GR], F16)
        hot_b = sb("hot_b", [P, 2, P, GR], F16)
        sg = sb("sg", [P, 2, NA, P])
        g_sb = sb("g_sb", [P, 2, 2 * 512])
        act_g = sb("act_g", [P, 2, 2, TPB * P])
        act_u = sb("act_u", [P, 2, TPB * P])
        ve2 = sb("ve2", [P, 2, TPB])
        r12 = sb("r12", [P, 2, TPB])
        ssq = sb("ssq", [P, 2 * TPB])
        rqk = sb("rqk", [P, 2 * TPB])
        nrq = sb("nrq", [P, TPB])
        table_one = sb("table_one", [P, 1])
        carrier = sb("carrier", [P, 16])
        stream = psum("stream", [P, 3, 512])
        gate = psum("gate", [P, 2, 2, 512])
        acc = psum("acc", [P, TPB, P])

        w_keys = sem("w_keys")
        w_early = sem("w_early")
        w_late = sem("w_late")
        key_hi = sem("key_hi")
        key_split = sem("key_split")
        whi = sem("whi")
        wsplit = sem("wsplit")
        pconst = sem("pconst")
        x_in0 = sem("x_in0")
        x_in1 = sem("x_in1")
        keyw_mm = sem("keyw_mm")
        stat_d = sem("stat_d")
        rstd_d = sem("rstd_d")
        xm0_d = sem("xm0_d")
        xn_d = sem("xn_d")
        xt_d = sem("xt_d")
        xcp_d = sem("xcp_d")
        xlo_d = sem("xlo_d")
        sim_mm = sem("sim_mm")
        sim_out = sem("sim_out")
        dn_mm = sem("dn_mm")
        dn_out = sem("dn_out")
        mlp_mm = sem("mlp_mm")
        mlp_out = sem("mlp_out")
        mlp_d = sem("mlp_d")
        top_d = sem("top_d")
        tail_d = sem("tail_d")
        exp_d = sem("exp_d")
        pick_d = sem("pick_d")
        v0_d = sem("v0_d")
        v_d = sem("v_d")
        vlo_d = sem("vlo_d")
        vbd0_in = sem("vbd0_in")
        vbd_in = sem("vbd_in")
        hot_d = sem("hot_d")
        g_mm = sem("g_mm")
        g_out = sem("g_out")
        sg_d = sem("sg_d")
        sg2_d = sem("sg2_d")
        up_mm = sem("up_mm")
        res_d = sem("res_d")
        out_d = sem("out_d")
        mstat_d = sem("mstat_d")
        r12_d = sem("r12_d")
        xm_d = sem("xm_d")
        z_d = sem("z_d")
        xs_d = sem("xs_d")
        zt_mm = sem("zt_mm")
        zt_out = sem("zt_out")
        qkv_mm = sem("qkv_mm")
        sq_d = sem("sq_d")
        ss_d = sem("ss_d")
        rqk_d = sem("rqk_d")
        nrq_d = sem("nrq_d")
        ek_d = sem("ek_d")
        eq_d = sem("eq_d")
        kv_d = sem("kv_d")
        prior_d = sem("prior_d")
        sum_mm = sem("sum_mm")
        y_d = sem("y_d")
        yt_mm = sem("yt_mm")
        yt_out = sem("yt_out")
        uv_mm = sem("uv_mm")
        silu_d = sem("silu_d")
        h_d = sem("h_d")
        ht_mm = sem("ht_mm")
        ht_out = sem("ht_out")
        o_mm = sem("o_mm")
        mix_d = sem("mix_d")

        block = ctx.enter_context(nc.Block())

        def wait(eng, s, value):
            if isinstance(value, int) and value <= 0:
                return
            eng.wait_ge(s, value)

        carried = [0]

        def wait_apart(dve, s, value):
            wait(dve, s, value)
            carried[0] += 1
            dve.memset(carrier[:, carried[0] % 16:carried[0] % 16 + 1], 0.0)

        def is_lead(n, base):
            return isinstance(n, int) and n == base - 2

        def schedule(eng, phase, body):
            base = phase * NB
            first = min(2, NB) if NB >= 6 else NB
            for n in range(-2, first):
                body(base, base + n, n >= 0, 0 <= n + 1 < NB, n + 2 < NB, (base + n) % 2)
            if first < NB:
                with eng.Fori(first // 2, NB // 2 - 1) as pair_no:
                    n = eng.snap(pair_no * 2 + base)
                    body(base, n, True, True, True, 0)
                    body(base, n + 1, True, True, True, 1)
                body(base, base + NB - 2, True, True, False, 0)
                body(base, base + NB - 1, True, False, False, 1)

        down_stage = sg[:, 0, :, :].rearrange("p a t -> p (a t)")
        stage = sg[:, 1, :, :].rearrange("p a t -> p (a t)")
        query_stage = stage[:, 0:2 * P].rearrange("p (s d) -> p s d", s=2)
        keys_stage = stage[:, 2 * P:4 * P].rearrange("p (s k) -> p s k", s=2)
        gu_stage = stage[:, 4 * P:8 * P]
        key_ps = [gate[:, :, :, s * NK:(s + 1) * NK].rearrange("p b c k -> p c b k") for s in range(2)]
        PLACE = {"sims 2": 0, "down 1": 2, "sims 3": 6, "down 2": 8, "down 3": 12, "turn": 16, "sims 0": 17,
                 "down 0": 19, "mlp": 23, "sims 1": 27}

        def bank(kind, j=0):
            return (PLACE[kind] + j) % 3

        turned = stream[:, bank("turn"), :]
        N_IDENT = 5
        N_CONST = 12
        steps = (["pairs_a", "pairs_b", "value_x", "value_y"] + ["score"] * (TPB * H) + ["pos"] * (TPB * H)
                 + ["shifted", "pick_x", "bits", "rank_y", "pick_y", "wsum", "picked", "winv", "a", "bclamp", "weight",
                    "b", "w_t", "a_t", "w_hi", "b_t", "w_lo", "hot_a"])
        TAIL = len(steps)

        def at(n, step):
            return TAIL * n + TAIL - steps[::-1].index(step)

        def flat(ap):
            return ap.rearrange("p t d -> p (t d)")

        def by_tile(ap):
            return ap.rearrange("p (t d) -> p t d", t=TPB)

        z_buf = by_tile(sim[:, 0, 0:512])
        z_t = sim[:, 0, 512:1024]
        e_q = by_tile(sim[:, 1, 0:512])
        y_buf = [by_tile(sim[:, 1, 512:1024]), by_tile(x_t[:])]
        spare = sg[:].rearrange("p b a t -> p (b a t)")
        squares = spare[:, 0:1024]
        prior = spare[:, 2048:3584].rearrange("p (n c d) -> p n c d", n=6, c=2)
        y_t = spare[:, 3584:4096]
        wkv = pick[:].rearrange("p s m k i -> p (s m k i)").rearrange("p (o c t d) -> p o c t d", o=2, c=2, t=TPB)
        s_gate = by_tile(act_g[:, 0, 0, :])
        h_t = act_g[:, 0, 1, :]
        banks = gate[:].rearrange("p h c f -> p (h c) f")
        qkv = [by_tile(banks[:, c, :]) for c in range(3)]
        u_ps = by_tile(banks[:, 3, :])
        sums = [by_tile(stream[:, c, :]) for c in range(3) if c != bank("turn")]

        def is_final(n, base):
            return base == 0 and isinstance(n, int) and n == NB - 1

        def mixing_step(body, i):
            body(i, i % 2, lambda j: 0 <= i + j < NB)

        def attention(eng, body, tail):
            def one(i):
                mixing_step(body, i)
                if i in tail:
                    tail[i]()
            first = 2 if NB >= 8 else NB + 2
            for i in range(first):
                one(i)
            if first == 2:
                pairs = (NB - 5) // 2
                with eng.Fori(1, pairs + 1) as row:
                    i = eng.snap(row * 2)
                    body(i, 0, lambda j: True)
                    body(i + 1, 1, lambda j: True)
                for i in range(2 * pairs + 2, NB + 2):
                    one(i)

        def attention_pe(pe):
            def turn_block(src):
                for t in range(TPB):
                    mm = pe.transpose(turned[:, t * P:(t + 1) * P], src[:, t, :], ident[:])
                return mm

            def running_sums(i, odd, ch):
                for t in range(TPB):
                    tile_no = TPB * odd + t
                    if odd or t >= 2:
                        pe.wait_ge(prior_d, 3 * i + (t if odd else t - 1))
                    mm = pe.matmul(sums[ch][:, t, :], tri[:], wkv[:, odd, ch, t, :], start=True, stop=tile_no == 0)
                    if tile_no:
                        before = wkv[:, odd, ch, 0, :] if tile_no == 1 else prior[:, tile_no - 2, ch, :]
                        mm = pe.matmul(sums[ch][:, t, :], ones[:], before, start=False, stop=True)
                return mm

            def body(i, odd, has):
                if has(1):
                    pe.wait_ge(zt_out, i + 2)
                    if has(0):
                        pe.wait_ge(eq_d, 5 * i + 4)
                        pe.wait_ge(kv_d, i + 1)
                    for ch in (1, 0, 2):
                        for t in range(TPB):
                            mm = pe.matmul(qkv[ch][:, t, :], z_t[:, t * P:(t + 1) * P],
                                           w_qkv[:, ch * P:(ch + 1) * P], start=True, stop=True)
                    mm.then_inc(qkv_mm, 1)
                if has(-2):
                    pe.wait_ge(h_d, i - 1)
                    turn_block(s_gate).then_inc(ht_mm, 1)
                if has(0):
                    pe.wait_ge(kv_d, i + 1)
                    wait(pe, y_d, 3 * i - 2)
                    running_sums(i, odd, 0).then_inc(sum_mm, 1)
                if has(-2):
                    pe.wait_ge(ht_out, i - 1)
                    for t in range(TPB):
                        mm = pe.matmul(acc[:, t, :], h_t[:, t * P:(t + 1) * P], w_o[:], start=True, stop=True)
                    mm.then_inc(o_mm, 1)
                if has(-1):
                    pe.wait_ge(y_d, 3 * i)
                    turn_block(y_buf[1 - odd]).then_inc(yt_mm, 1)
                if has(0):
                    wait(pe, y_d, 3 * i)
                    running_sums(i, odd, 1).then_inc(sum_mm, 1)
                if has(2):
                    pe.wait_ge(z_d, i + 3)
                    wait(pe, yt_out, i)
                    turn_block(z_buf).then_inc(zt_mm, 1)
                if has(-1):
                    pe.wait_ge(yt_out, i)
                    wait(pe, mix_d, i - 1)
                    for dst, w in ((acc, 1), (u_ps, 0)):
                        for t in range(TPB):
                            mm = pe.matmul(dst[:, t, :], y_t[:, t * P:(t + 1) * P], w_sw[:, w * P:(w + 1) * P],
                                           start=True, stop=True)
                    mm.then_inc(uv_mm, 1)

            return body

        def attention_act(act):
            def body(i, odd, has):
                if has(1):
                    act.activation(table_one[:], ones[:, 0:1], ACT.Exp)
                    act.wait_ge(qkv_mm, i + 2)
                    wait(act, ss_d, 2 * (i + 1))
                    act.activation(squares, banks[:, 0:2, :].rearrange("p c f -> p (c f)"), ACT.Square).then_inc(sq_d, 1)
                if has(-2):
                    act.wait_ge(ht_mm, i - 1)
                    act.copy(h_t, turned).then_inc(ht_out, 1)
                if has(-1):
                    act.wait_ge(yt_mm, i)
                    act.copy(y_t, turned).then_inc(yt_out, 1)
                if has(1):
                    m = i + 1
                    act.wait_ge(rqk_d, m + 1)
                    wait(act, sum_mm, 2 * (m - 1))
                    wait(act, prior_d, 3 * (m - 1))
                    for t in range(TPB):
                        act.activation(wkv[:, 1 - odd, 0, t, :], qkv[1][:, t, :], ACT.Exp,
                                       scale=rqk[:, TPB + t:TPB + t + 1]).then_inc(ek_d, 1)
                    act.wait_ge(nrq_d, m + 1)
                    wait(act, y_d, 3 * m - 2)
                    for t in range(TPB):
                        act.activation(e_q[:, t, :], qkv[0][:, t, :], ACT.Exp, scale=nrq[:, t:t + 1]).then_inc(eq_d, 1)
                    act.wait_ge(eq_d, 5 * m + 4)
                    act.activation(flat(e_q), flat(e_q), ACT.Copy, bias=1.0).then_inc(eq_d, 1)
                if has(2):
                    act.wait_ge(zt_mm, i + 3)
                    act.copy(z_t, turned).then_inc(zt_out, 1)
                if has(-1):
                    act.wait_ge(uv_mm, i)
                    wait(act, ht_mm, i - 1)
                    act.activation(flat(s_gate), flat(acc[:]), ACT.Silu).then_inc(silu_d, 1)

            return body

        def attention_pool(pool):
            def body(i, odd, has):
                if has(0):
                    pool.wait_ge(kv_d, i + 1)
                    wait(pool, sum_mm, 2 * (i - 1) if odd else 2 * i)
                    first = TPB - 1 if odd else 0
                    for t in range(first, first + 3):
                        wait(pool, prior_d, 3 * i + t - first)
                        pool.tensor_tensor(prior[:, t], prior[:, t - 1] if t else wkv[:, odd, :, 0, :],
                                           wkv[:, odd, :, t - first + 1 - odd, :], ALU.add).then_inc(prior_d, 1)
                if has(2):
                    pool.wait_ge(xm_d, i + 3)
                    wait(pool, zt_mm, i + 2)
                    pool.tensor_tensor(z_buf, xn[:], r12[:, 1, :, None].broadcast_to([P, TPB, P]), ALU.mult).then_inc(z_d, 1)
                if has(1):
                    pool.wait_ge(ss_d, 2 * i + 4)
                    wait(pool, eq_d, 5 * i + 4)
                    pool.tensor_tensor(rqk[:], ssq[:], mhalf[:], ALU.pow).then_inc(rqk_d, 1)
                    pool.wait_ge(rqk_d, i + 2)
                    pool.tensor_tensor(nrq[:], rqk[:, 0:TPB], minus[:], ALU.mult).then_inc(nrq_d, 1)
                if has(2):
                    xv = x_all[:, bass.ds((i + 2) * TPB, TPB), :]
                    pool.tensor_tensor(xv, xv, xn[:], ALU.add).then_inc(xs_d, 1)
                if has(3):
                    pool.wait_ge(mstat_d, 12 * i + 48)
                    wait(pool, z_d, i + 3)
                    pool.tensor_tensor(r12[:].rearrange("p c t -> p (c t)"), ve2[:].rearrange("p c t -> p (c t)"), mhalf[:],
                                       ALU.pow).then_inc(r12_d, 1)

            return body

        def attention_dve(dve):
            def body(i, odd, has):
                y = y_buf[odd]
                if has(0):
                    dve.wait_ge(ek_d, 4 * i + 4)
                    dve.tensor_tensor(wkv[:, odd, 1], wkv[:, odd, 0], qkv[2], ALU.mult).then_inc(kv_d, 1)
                if has(-2):
                    dve.wait_ge(silu_d, i - 1)
                    dve.tensor_tensor(s_gate, s_gate, u_ps, ALU.mult).then_inc(h_d, 1)
                if has(2):
                    m = i + 2
                    dve.wait_ge(r12_d, m + 1)
                    wait(dve, xs_d, m)
                    for t in range(TPB):
                        ins = dve.tensor_scalar(xn[:, t, :], x_all[:, m * TPB + t, :], mv[:, t, 0:1],
                                                r12[:, 0, t:t + 1], ALU.subtract, ALU.mult)
                    ins.then_inc(xm_d, 1)
                if has(3):
                    m = i + 3
                    wait(dve, r12_d, m)
                    for t in range(TPB):
                        dve.bn_stats(stats[:, t, :], x_all[:, m * TPB + t, :]).then_inc(mstat_d, 1)
                    wait_apart(dve, mstat_d, 12 * m + TPB)
                    for t in range(TPB):
                        dve.bn_aggr(mv[:, t, :], stats[:, t, :]).then_inc(mstat_d, 1)
                    dve.wait_ge(mstat_d, 12 * m + 8)
                    dve.tensor_scalar(ve2[:, 0, :], mv[:, :, 1], LN_EPS, None, ALU.add).then_inc(mstat_d, 1)
                    dve.wait_ge(mstat_d, 12 * m + 9)
                    dve.reciprocal(ve2[:, 1, :], ve2[:, 0, :]).then_inc(mstat_d, 1)
                    dve.wait_ge(mstat_d, 12 * m + 10)
                    dve.tensor_tensor(ve2[:, 1, :], ve2[:, 1, :], mv[:, :, 1], ALU.mult).then_inc(mstat_d, 1)
                    dve.wait_ge(mstat_d, 12 * m + 11)
                    dve.tensor_scalar(ve2[:, 1, :], ve2[:, 1, :], RMS_EPS, None, ALU.add).then_inc(mstat_d, 1)
                if has(1):
                    m = i + 1
                    dve.wait_ge(sq_d, m + 1)
                    wait(dve, rqk_d, m)
                    dve.tensor_reduce(ssq[:], squares.rearrange("p (n d) -> p n d", d=P), AX.X, ALU.add).then_inc(ss_d, 1)
                    dve.wait_ge(ss_d, 2 * m + 1)
                    dve.tensor_scalar(ssq[:], ssq[:], 1.0 / P, RMS_EPS, ALU.mult, ALU.add).then_inc(ss_d, 1)
                if has(0):
                    dve.wait_ge(sum_mm, 2 * i + 1)
                    dve.wait_ge(eq_d, 5 * i + 5)
                    wait(dve, yt_mm, i - 1)
                    dve.scalar_tensor_tensor(y, sums[0], CUM_EPS, e_q, ALU.add, ALU.mult).then_inc(y_d, 1)
                if has(-2):
                    m = i - 2
                    dve.wait_ge(o_mm, m + 1)
                    dve.wait_ge(xs_d, m + 1)
                    xv = x_all[:, bass.ds(m * TPB, TPB), :]
                    dve.tensor_tensor(xv, xv, acc[:], ALU.add).then_inc(mix_d, 1)
                if has(0):
                    dve.wait_ge(y_d, 3 * i + 1)
                    dve.reciprocal(y, y).then_inc(y_d, 1)
                    dve.wait_ge(y_d, 3 * i + 2)
                    dve.wait_ge(sum_mm, 2 * i + 2)
                    dve.tensor_tensor(y, y, sums[1], ALU.mult).then_inc(y_d, 1)

            return body

        @block.sync
        def _(sp):
            nx = min(2 * TPB, NT)
            sp.dma_start(x_all[:, 0:nx, :], x_dram[:, 0:nx, :]).then_inc(x_in0, 16)
            sp.dma_start(query_stage, w_queries.rearrange("(s r) d -> r s d", s=2)).then_inc(w_keys, 16)
            sp.dma_start(keys_stage, keys_t.rearrange("s r k -> r s k")).then_inc(w_keys, 16)
            sp.dma_start(gu_stage, w_gu_t).then_inc(w_early, 16)
            sp.dma_start(down_stage, down_t).then_inc(w_early, 16)
            sp.dma_start(upw[:], up.rearrange("(a b) d -> b a d", b=P)).then_inc(w_late, 16)
            sp.dma_start(wdn[:], w_down_t.rearrange("(c u) d -> u c d", c=2)).then_inc(w_late, 16)
            sp.dma_start(w_qkv[:], w_qkv_t).then_inc(w_late, 16)
            sp.dma_start(w_sw[:], w_swiglu_t).then_inc(w_late, 16)
            sp.dma_start(w_o[:], w_out_t).then_inc(w_late, 16)
            if NT > nx:
                sp.dma_start(x_all[:, nx:, :], x_dram[:, nx:, :]).then_inc(x_in1, 16)

            def body(base, n, cur, nxt, second, odd):
                if nxt:
                    sp.wait_ge(v0_d, n + 2)
                    for q in range(Q):
                        r = slice(32 * q, 32 * q + 32)
                        sp.dma_start(vbd[r, 0, q], vw[r, 0]).then_inc(vbd0_in, 16)
                    sp.wait_ge(v_d, n + 2)
                    sp.wait_ge(vlo_d, n + 2)
                    for q in range(Q):
                        r = slice(32 * q, 32 * q + 32)
                        sp.dma_start(vbd[r, 1:TPB, q], vw[r, 1:TPB]).then_inc(vbd_in, 16)
                if cur and base > 0:
                    t = (n - base) * TPB
                    sp.wait_ge(res_d, n + 1)
                    sp.dma_start(out_dram[:, bass.ds(t, TPB), :], x_all[:, bass.ds(t, TPB), :]).then_inc(out_d, 16)

            schedule(sp, 0, body)
            schedule(sp, 1, body)
            sp.wait_ge(out_d, 16 * NB)

        @block.tensor
        def _(pe):
            mixing = attention_pe(pe)

            def prepare():
                pe.wait_ge(w_keys, 32)
                for s in range(2):
                    for h in range(H):
                        r = slice(32 * h, 32 * h + 32)
                        mm = pe.matmul(gate[:, h % 2, h // 2, s * NK:(s + 1) * NK],
                                       query_stage[r, s, :], keys_stage[r, s, :], start=True, stop=True)
                mm.then_inc(keyw_mm, 1)

            def turn(n):
                pe.wait_ge(xn_d, n + 1)
                for t in range(TPB):
                    mm = pe.transpose(turned[:, t * P:(t + 1) * P], xn[:, t, :], ident[:])
                mm.then_inc(xt_d, 1)

            def sims(n, t, odd, empty):
                pe.wait_ge(xlo_d, n + 1)
                tok = slice(t * P, (t + 1) * P)
                for j in range(2):
                    o = empty(f"sims {t}", j)
                    key = slice(j * 512, (j + 1) * 512)
                    pe.matmul(o, xs[:, odd, 0, tok], keyw[:, 0, key], start=True, stop=False)
                    pe.matmul(o, xs[:, odd, 0, tok], keyw[:, 1, key], start=False, stop=False)
                    pe.matmul(o, xs[:, odd, 1, tok], keyw[:, 0, key], start=False,
                              stop=True).then_inc(sim_mm, 1)

            def experts_down(n, t, odd, empty):
                tok = slice(t * P, (t + 1) * P)
                for j in range(4):
                    group = empty(f"down {t}", j)
                    for a in range(4 * j, 4 * j + 4):
                        o = group[:, (a % 4) * P:(a % 4 + 1) * P]
                        e = slice(a * P, (a + 1) * P)
                        pe.matmul(o, down[:, 0, e], xs[:, odd, 0, tok], start=True, stop=False)
                        pe.matmul(o, down[:, 0, e], xs[:, odd, 1, tok], start=False, stop=False)
                        mm = pe.matmul(o, down[:, 1, e], xs[:, odd, 0, tok], start=False, stop=True)
                    mm.then_inc(dn_mm, 1)

            def mlp_up(n, odd, empty):
                for j in range(4):
                    o = empty("mlp", j)
                    u = slice(j * P, (j + 1) * P)
                    pe.matmul(o, wgu[:, 0, u], xs[:, odd, 0, :], start=True, stop=False)
                    pe.matmul(o, wgu[:, 0, u], xs[:, odd, 1, :], start=False, stop=False)
                    pe.matmul(o, wgu[:, 1, u], xs[:, odd, 0, :], start=False, stop=True).then_inc(mlp_mm, 1)

            def gates(n, t):
                if t < 2:
                    pe.wait_ge(vbd_in if t else vbd0_in, 64 * (n + 1))
                pe.wait_ge(hot_d, 4 * n + t + 1)
                for h in range(2):
                    wait(pe, g_out if h else sg_d, 4 * n + t)
                    for i in range(16):
                        g = 16 * h + i
                        o = gate[:, h, i // 8, (i % 8) * 64:(i % 8 + 1) * 64]
                        for part in range(2):
                            mm = pe.matmul(o, hot_b[:, t % 2, :, g],
                                           vbd[:, t, :, part, :, g],
                                           start=(part == 0), stop=(part == 1))
                    mm.then_inc(g_mm, 1)

            def experts_up(n, t, odd):
                if t == 0:
                    wait(pe, res_d, n)
                    pe.wait_ge(mlp_d, n + 1)
                tok = slice(t * P, (t + 1) * P)
                for c in range(2):
                    pe.matmul(acc[:, t, :], act_g[:, odd, c, tok], wdn[:, c, :], start=(c == 0), stop=False)
                pe.wait_ge(sg_d, 4 * n + t + 1)
                pe.wait_ge(sg2_d, 4 * n + t + 1)
                for a in range(NA):
                    mm = pe.matmul(acc[:, t, :], sg[:, t % 2, a, :], upw[:, a, :], start=False, stop=(a == NA - 1))
                mm.then_inc(up_mm, 1)

            def taken_out(n, base, cur, nxt, second):
                there = []
                if is_lead(n, base):
                    there += [(PLACE["turn"], xcp_d, 2 * (n + 2) + 2)]
                if nxt:
                    there += [(PLACE["sims 2"] + j, sim_out, 8 * (n + 1) + 5 + j) for j in range(2)]
                if cur:
                    there += [(PLACE["down 1"] + j, dn_out, 16 * n + 5 + j) for j in range(4)]
                if nxt:
                    there += [(PLACE["sims 3"] + j, sim_out, 8 * (n + 1) + 7 + j) for j in range(2)]
                if cur:
                    there += [(PLACE["down 2"] + j, dn_out, 16 * n + 9 + j) for j in range(8)]
                if second and not is_lead(n, base):
                    there += [(PLACE["turn"], xcp_d, 2 * (n + 2) + 2)]
                if second:
                    there += [(PLACE["sims 0"] + j, sim_out, 8 * (n + 2) + 1 + j) for j in range(2)]
                if nxt:
                    there += [(PLACE["down 0"] + j, dn_out, 16 * (n + 1) + 1 + j) for j in range(4)]
                    there += [(PLACE["mlp"] + j, mlp_out, 4 * (n + 1) + 1 + j) for j in range(4)]
                if second:
                    there += [(PLACE["sims 1"] + j, sim_out, 8 * (n + 2) + 3 + j) for j in range(2)]
                return there

            def body(base, n, cur, nxt, second, odd):
                first = isinstance(n, int) and n - base < 0
                before = [] if is_lead(n, base) else taken_out(n - 1, base, cur and not (isinstance(n, int) and n == base),
                                                               not first, nxt)
                now = taken_out(n, base, cur, nxt, second)

                def empty(kind, j=0):
                    place = PLACE[kind] + j
                    earlier = before + [g for g in now if g[0] < place or (is_lead(n, base) and g[0] == PLACE["turn"])]
                    same = [g for g in earlier if g[0] % 3 == place % 3]
                    if same:
                        pe.wait_ge(same[-1][1], same[-1][2])
                    return stream[:, place % 3, :]

                if nxt:
                    sims(n + 1, 2, 1 - odd, empty)
                if cur:
                    experts_down(n, 1, odd, empty)
                    gates(n, 0)
                if nxt:
                    sims(n + 1, 3, 1 - odd, empty)
                if cur:
                    gates(n, 1)
                    experts_up(n, 0, odd)
                    experts_down(n, 2, odd, empty)
                    experts_up(n, 1, odd)
                if cur:
                    gates(n, 2)
                    experts_down(n, 3, odd, empty)
                if second and not is_lead(n, base):
                    empty("turn")
                    turn(n + 2)
                if cur:
                    experts_up(n, 2, odd)
                if cur:
                    gates(n, 3)
                if second:
                    sims(n + 2, 0, odd, empty)
                if isinstance(n, int) and n == -1:
                    pe.wait_ge(wsplit, 2)
                    pe.wait_ge(w_late, 16 * 5)
                if nxt:
                    experts_down(n + 1, 0, 1 - odd, empty)
                    mlp_up(n + 1, 1 - odd, empty)
                if second:
                    sims(n + 2, 1, odd, empty)
                if is_final(n, base):
                    pe.wait_ge(dn_out, 16 * NB)
                    mixing_step(mixing, -2)
                    pe.wait_ge(sg_d, 4 * NB)
                    pe.wait_ge(g_out, 4 * NB)
                    mixing_step(mixing, -1)
                if cur:
                    experts_up(n, 3, odd)

            prepare()
            pe.wait_ge(pconst, N_IDENT)
            turn(0)
            pe.wait_ge(key_split, 2)
            schedule(pe, 0, body)

            def turn_next():
                turn(NB)
                pe.wait_ge(xcp_d, 2 * NB + 2)

            attention(pe, mixing, {NB: turn_next})
            schedule(pe, 1, body)

        @block.scalar
        def _(act):
            mixing = attention_act(act)

            def take_sims(m, t):
                wait(act, top_d, 16 * (4 * m + t - 1))
                for j in range(2):
                    act.wait_ge(sim_mm, 8 * m + 2 * t + j + 1)
                    act.copy(sim[:, t % 2, j * 512:(j + 1) * 512], stream[:, bank(f"sims {t}", j), :]).then_inc(sim_out, 1)

            def take_down(m, t):
                wait(act, up_mm, 4 * m + t - 1)
                for j in range(4):
                    act.wait_ge(dn_mm, 16 * m + 4 * t + j + 1)
                    act.activation(sg[:, t % 2, 4 * j:4 * j + 4, :].rearrange("p a t -> p (a t)"),
                                   stream[:, bank(f"down {t}", j), :], ACT.Silu).then_inc(dn_out, 1)

            def take_gates(n, t):
                act.wait_ge(g_mm, 8 * n + 2 * t + 2)
                wait(act, sg2_d, 4 * n + t - 1)
                act.copy(g_sb[:, t % 2, :], gate[:, 1].rearrange("p c f -> p (c f)")).then_inc(g_out, 1)

            def take_mlp(m, odd):
                wait(act, up_mm, 4 * (m - 1))
                wait(act, mlp_d, m)
                for j in range(4):
                    act.wait_ge(mlp_mm, 4 * m + j + 1)
                    o = stream[:, bank("mlp", j), :]
                    if j < 2:
                        act.activation(act_g[:, odd, j, :], o, ACT.Silu).then_inc(mlp_out, 1)
                    else:
                        act.copy(act_u[:, j - 2, :], o).then_inc(mlp_out, 1)

            def take_turned(m, odd):
                act.wait_ge(xt_d, m + 1)
                act.copy(xs[:, odd, 0, :], turned).then_inc(xcp_d, 1)
                wait(act, xlo_d, m)
                act.copy(x_t[:], turned).then_inc(xcp_d, 1)

            def body(base, n, cur, nxt, second, odd):
                if isinstance(n, int) and n == -1:
                    act.wait_ge(w_early, 32)
                    act.copy(down[:, 0, :], down_stage).then_inc(whi, 1)
                    act.copy(wgu[:, 0, :], gu_stage).then_inc(whi, 1)
                for t in range(TPB):
                    if t == TPB - 1 and nxt:
                        act.wait_ge(tail_d, at(n + 1, "shifted"))
                        act.activation(wexp[:], wexp[:], ACT.Exp).then_inc(exp_d, 1)
                        act.activation(table_one[:], ones[:, 0:1], ACT.Silu)
                    if t > 0 and cur:
                        take_gates(n, t)
                    if t == 0 and nxt:
                        take_sims(n + 1, 2)
                    if t == TPB - 1 and is_final(n, base):
                        mixing_step(mixing, -2)
                        mixing_step(mixing, -1)
                    if t < TPB - 1:
                        if cur:
                            take_down(n, t + 1)
                            if t == 0:
                                take_gates(n, t)
                        if t == 0 and nxt:
                            take_sims(n + 1, 3)
                        if t == TPB - 2 and second and not is_lead(n, base):
                            take_turned(n + 2, odd)
                        continue
                    if second:
                        take_sims(n + 2, 0)
                    if nxt:
                        take_down(n + 1, 0)
                        take_mlp(n + 1, 1 - odd)
                    if second:
                        take_sims(n + 2, 1)

            act.wait_ge(keyw_mm, 1)
            for s in range(2):
                hi = keyw[:, 0, :].rearrange("p (s h2 h1 k) -> p s h2 h1 k", s=2, h2=2, h1=2)[:, s]
                act.copy(hi, key_ps[s]).then_inc(key_hi, 1)
            take_turned(0, 0)
            schedule(act, 0, body)
            attention(act, mixing, {NB: lambda: take_turned(NB, NB % 2)})
            schedule(act, 1, body)

        @block.gpsimd
        def _(pool):
            pool.memset(mhalf[:], -0.5).then_inc(pconst, 1)
            pool.memset(ones[:], 1.0).then_inc(pconst, 1)
            pool.memset(minus[:], -1.0).then_inc(pconst, 1)
            pool.wait_ge(pconst, 2)
            pool.affine_select(out=tri[:], in_=ones[:], compare_op=ALU.is_ge, fill=0.0, base=0,
                               pattern=[[1, P]], channel_multiplier=-1).then_inc(pconst, 1)
            pool.affine_select(out=ident[:], in_=ones[:], compare_op=ALU.is_equal, fill=0.0, base=0,
                               pattern=[[1, P]], channel_multiplier=-1).then_inc(pconst, 1)

            def deviation(m):
                pool.wait_ge(stat_d, 9 * m + 9)
                pool.tensor_tensor(rstd[:], veps[:], mhalf[:, 0:TPB], ALU.pow).then_inc(rstd_d, 1)

            def normalise(m, base):
                wait(pool, xt_d, m)
                x = x_all[:, bass.ds((m - base) * TPB, TPB), :]
                wide = [P, TPB, P]
                pool.tensor_tensor(xn[:], x, mv[:, :, 0:1].broadcast_to(wide), ALU.subtract).then_inc(xm0_d, 1)
                pool.wait_ge(rstd_d, m + 1)
                pool.wait_ge(xm0_d, m + 1)
                pool.tensor_tensor(xn[:], xn[:], rstd[:, :, None].broadcast_to(wide), ALU.mult).then_inc(xn_d, 1)

            def low_part(m, odd):
                pool.wait_ge(xcp_d, 2 * m + 2)
                pool.tensor_tensor(xs[:, odd, 1, :], x_t[:], xs[:, odd, 0, :], ALU.subtract).then_inc(xlo_d, 1)

            pool.wait_ge(pconst, N_IDENT)
            deviation(0)
            normalise(0, 0)
            pool.iota(iota_k[:], [[1, K]], base=0, channel_multiplier=0,
                      allow_small_or_imprecise_dtypes=True).then_inc(pconst, 1)
            pool.iota(iota_a[:], [[1, NA], [0, GR]], base=0, channel_multiplier=0,
                      allow_small_or_imprecise_dtypes=True).then_inc(pconst, 1)
            pool.iota(first_pair[:, 0:2], [[K, 2]], base=0, channel_multiplier=0,
                      allow_small_or_imprecise_dtypes=True).then_inc(pconst, 1)
            pool.iota(first_pair[:, 2:K], [[2, K - 2]], base=2 * K, channel_multiplier=0,
                      allow_small_or_imprecise_dtypes=True).then_inc(pconst, 1)
            pool.memset(idx_x[:, :, 0], 0).then_inc(pconst, 1)
            low_part(0, 0)
            pool.iota(iota_b[:], [[1, P], [0, GR]], base=0, channel_multiplier=0,
                      allow_small_or_imprecise_dtypes=True).then_inc(pconst, 1)
            pool.memset(vbd[:].rearrange("p t q h a g -> p (t q h a g)").bitcast(U32), 0).then_inc(pconst, 1)
            pool.wait_ge(pconst, N_CONST)

            def second_half(ap):
                return ap.rearrange("p a (q g) -> p a q g", q=Q)[:, :, :, GR // 2:]

            def weigh(n, t):
                pool.wait_ge(dn_out, 16 * n + 4 * t + 4)
                pool.wait_ge(g_out, 4 * n + t + 1)
                s = second_half(sg[:, t % 2])
                g = g_sb[:, t % 2].rearrange("p (g q a) -> p a q g", q=Q, a=NA)
                pool.tensor_tensor(s, s, g, ALU.mult).then_inc(sg2_d, 1)

            def body(base, n, cur, nxt, second, odd):
                if cur:
                    weigh(n, 0)
                if is_final(n, base):
                    mixing_step(mixing, -3)
                if second and not is_lead(n, base):
                    deviation(n + 2)
                if cur:
                    weigh(n, 1)
                if second and not is_lead(n, base):
                    normalise(n + 2, base)
                if cur:
                    if is_final(n, base):
                        mixing_step(mixing, -2)
                    weigh(n, 2)
                if second and not is_lead(n, base):
                    low_part(n + 2, odd)
                if nxt:
                    m = n + 1
                    for s, step in enumerate(("pick_x", "pick_y")):
                        pool.wait_ge(tail_d, at(m, step))
                        pool.tensor_tensor(pick[:, s], pick[:, s],
                                           value[:, s, :, None, :].broadcast_to([P, TPB * H, K, K]),
                                           ALU.mult).then_inc(pick_d, 1)
                    pool.wait_ge(pick_d, 3 * m + 2)
                    halves = pick[:].rearrange("p s m k i -> p (s m k) i")
                    pool.tensor_tensor(halves[:, :, 0:K // 2], halves[:, :, 0:K // 2], halves[:, :, K // 2:K],
                                       ALU.add).then_inc(pick_d, 1)
                if cur:
                    weigh(n, 3)
                if is_final(n, base):
                    mixing_step(mixing, -1)
                if nxt:
                    pool.wait_ge(mlp_out, 4 * m + 4)
                    g = act_g[:, 1 - odd].rearrange("p c t -> p (c t)")
                    pool.tensor_tensor(g, g, act_u[:].rearrange("p c t -> p (c t)"), ALU.mult).then_inc(mlp_d, 1)
                    pool.wait_ge(tail_d, at(m, "hot_a"))
                    wait(pool, vbd_in, 64 * m)
                    for t in range(1, TPB):
                        ins = pool.tensor_tensor(vw[:, t, 1], hot_a[:, t],
                                                 w_hl[:, 1, None, t * GR:(t + 1) * GR].broadcast_to([P, NA, GR]), ALU.mult)
                    ins.then_inc(vlo_d, 1)

            mixing = attention_pool(pool)
            schedule(pool, 0, body)
            attention(pool, mixing, {})
            deviation(NB)
            normalise(NB, NB)
            low_part(NB, NB % 2)
            schedule(pool, 1, body)

        @block.vector
        def _(dve):
            mixing = attention_dve(dve)

            def block_of(n, base):
                return bass.ds((n - base) * TPB, TPB)

            def statistics(n, base):
                if base == 0:
                    if isinstance(n, int) and n < 2:
                        dve.wait_ge(x_in0, 16)
                    else:
                        dve.wait_ge(x_in1, 16)
                wait(dve, xn_d, n)
                for t in range(TPB):
                    dve.bn_stats(stats[:, t, :], x_all[:, (n - base) * TPB + t, :]).then_inc(stat_d, 1)
                wait_apart(dve, stat_d, 9 * n + TPB)
                for t in range(TPB):
                    dve.bn_aggr(mv[:, t, :], stats[:, t, :]).then_inc(stat_d, 1)
                dve.wait_ge(stat_d, 9 * n + 8)
                dve.tensor_scalar(veps[:], mv[:, :, 1], LN_EPS, None, ALU.add).then_inc(stat_d, 1)

            def search(n, t):
                wait_apart(dve, sim_out, 8 * n + 2 * t + 2)
                views = [(top[:, s, t * H + h, :], idx_y[:, t * H + h, :] if s else idx_x[:, t * H + h, 1:1 + K],
                          sim[:, t % 2, (s * H + h) * NK:(s * H + h + 1) * NK]) for s in range(2) for h in range(H)]
                for best, _, keys in views:
                    dve.max(best, keys).then_inc(top_d, 1)
                wait_apart(dve, top_d, 64 * n + 16 * t + 2 * H)
                for best, where, keys in views:
                    dve.max_index(where, best, keys).then_inc(top_d, 1)

            def select(n):
                every = [P, TPB * H, K, K]
                dve.wait_ge(top_d, 64 * n + 64)
                x, y = top[:, 0], top[:, 1]
                dve.tensor_tensor(pair[:, :, 0:2 * K].rearrange("p m (i j) -> p m i j", i=2),
                                  x[:, :, 0:2, None].broadcast_to([P, TPB * H, 2, K]),
                                  y[:, :, None, :].broadcast_to([P, TPB * H, 2, K]), ALU.add).then_inc(tail_d, 1)
                dve.tensor_tensor(pair[:, :, 2 * K:NP].rearrange("p m (i j) -> p m i j", j=2),
                                  x[:, :, 2:K, None].broadcast_to([P, TPB * H, K - 2, 2]),
                                  y[:, :, None, 0:2].broadcast_to([P, TPB * H, K - 2, 2]), ALU.add).then_inc(tail_d, 1)
                dve.tensor_tensor(value[:, 0], idx_x[:, :, 1:1 + K], idx_x[:, :, 0:K], ALU.subtract).then_inc(tail_d, 1)
                dve.tensor_copy(value[:, 1], idx_y[:]).then_inc(tail_d, 1)
                wait_apart(dve, tail_d, at(n, "pairs_b"))
                for m in range(TPB * H):
                    dve.max(score[:, m, :], pair[:, m, :]).then_inc(tail_d, 1)
                wait_apart(dve, tail_d, at(n, "score"))
                for m in range(TPB * H):
                    dve.max_index(pos[:, m, :], score[:, m, :], pair[:, m, :]).then_inc(tail_d, 1)
                dve.tensor_tensor(wexp[:], score[:], score[:, :, 0:1].broadcast_to([P, TPB * H, K]),
                                  ALU.subtract).then_inc(tail_d, 1)
                dve.wait_ge(tail_d, at(n, "pos"))
                dve.tensor_tensor(pick[:, 0], pos[:, :, :, None].broadcast_to(every),
                                  first_pair[:, None, None, :].broadcast_to(every), ALU.is_ge).then_inc(tail_d, 1)
                dve.tensor_scalar(bits[:], pos[:], float(2 * K), 6.0, ALU.is_lt, ALU.mult).then_inc(tail_d, 1)
                dve.wait_ge(tail_d, at(n, "bits"))
                dve.scalar_tensor_tensor(rank_y[:], bits[:], 1, pos[:], ALU.bitwise_or, ALU.bitwise_and).then_inc(tail_d, 1)
                dve.wait_ge(tail_d, at(n, "rank_y"))
                dve.tensor_tensor(pick[:, 1], rank_y[:, :, :, None].broadcast_to(every),
                                  iota_k[:, None, None, :].broadcast_to(every), ALU.is_equal).then_inc(tail_d, 1)

            def spread(n, odd):
                flat = "p m k -> p (m k)"
                dve.wait_ge(exp_d, n + 1)
                dve.tensor_reduce(wsum[:], wexp[:], AX.X, ALU.add).then_inc(tail_d, 1)
                dve.wait_ge(pick_d, 3 * n + 3)
                dve.tensor_reduce(picked[:], pick[:, :, :, :, 0:K // 2].rearrange("p s m k i -> p (s m k) i"), AX.X,
                                  ALU.add).then_inc(tail_d, 1)
                dve.wait_ge(tail_d, at(n, "wsum"))
                dve.reciprocal(wsum[:], wsum[:]).then_inc(tail_d, 1)
                dve.wait_ge(tail_d, at(n, "picked"))
                dve.tensor_scalar(ab[:, 0, :], picked[:, 0].rearrange(flat), float(NA - 1), None, ALU.min).then_inc(tail_d, 1)
                dve.tensor_scalar(bclamp[:], picked[:, 0].rearrange(flat), float(NA), float(P - 1), ALU.is_ge,
                                  ALU.mult).then_inc(tail_d, 1)
                dve.wait_ge(tail_d, at(n, "winv"))
                dve.tensor_tensor(wexp[:], wexp[:], wsum[:, :, None].broadcast_to([P, TPB * H, K]),
                                  ALU.mult).then_inc(tail_d, 1)
                dve.wait_ge(tail_d, at(n, "bclamp"))
                dve.tensor_tensor(ab[:, 1, :], bclamp[:], picked[:, 1].rearrange(flat), ALU.max).then_inc(tail_d, 1)
                dve.wait_ge(tail_d, at(n, "weight"))
                dve.transpose(w_t[:], wexp[:].rearrange(flat)).then_inc(tail_d, 1)
                dve.transpose(a_t[:], ab[:, 0, :]).then_inc(tail_d, 1)
                dve.wait_ge(tail_d, at(n, "w_t"))
                dve.tensor_copy(w_hl[:, 0, :], w_t[:]).then_inc(tail_d, 1)
                dve.transpose(b_t[:, odd, :], ab[:, 1, :]).then_inc(tail_d, 1)
                dve.wait_ge(tail_d, at(n, "w_hi"))
                dve.tensor_tensor(w_hl[:, 1, :], w_t[:], w_hl[:, 0, :], ALU.subtract).then_inc(tail_d, 1)
                wait(dve, vlo_d, n)
                dve.tensor_tensor(hot_a[:], iota_a[:, None].broadcast_to([P, TPB, NA, GR]),
                                  a_t[:].rearrange("p (t g) -> p t g", t=TPB)[:, :, None, :].broadcast_to([P, TPB, NA, GR]),
                                  ALU.is_equal).then_inc(tail_d, 1)
                dve.wait_ge(tail_d, at(n, "hot_a"))
                wait(dve, vbd0_in, 64 * n)
                for part in range(2):
                    ins = dve.tensor_tensor(vw[:, 0, part], hot_a[:, 0], w_hl[:, part, None, 0:GR].broadcast_to([P, NA, GR]),
                                            ALU.mult)
                ins.then_inc(v0_d, 1)
                wait(dve, vbd_in, 64 * n)
                for t in range(1, TPB):
                    ins = dve.tensor_tensor(vw[:, t, 0], hot_a[:, t],
                                            w_hl[:, 0, None, t * GR:(t + 1) * GR].broadcast_to([P, NA, GR]), ALU.mult)
                ins.then_inc(v_d, 1)

            def one_hot(n, t, odd):
                wait(dve, g_mm, 8 * n + 2 * t - 2)
                dve.tensor_tensor(hot_b[:, t % 2], iota_b[:],
                                  b_t[:, odd, None, t * GR:(t + 1) * GR].broadcast_to([P, P, GR]),
                                  ALU.is_equal).then_inc(hot_d, 1)

            def weigh(n, t):
                dve.wait_ge(dn_out, 16 * n + 4 * t + 4)
                dve.wait_ge(g_mm, 8 * n + 2 * t + 1)
                s = sg[:, t % 2].rearrange("p a (q g) -> p a q g", q=Q)[:, :, :, 0:GR // 2]
                g = gate[:, 0].rearrange("p c f -> p (c f)").rearrange("p (g q a) -> p a q g", q=Q, a=NA)
                dve.tensor_tensor(s, s, g, ALU.mult).then_inc(sg_d, 1)

            def residual(n, base):
                dve.wait_ge(up_mm, 4 * n + 4)
                xv = x_all[:, block_of(n, base), :]
                dve.scalar_tensor_tensor(xv, acc[:], 0.5, xv, ALU.mult, ALU.add).then_inc(res_d, 1)

            def body(base, n, cur, nxt, second, odd):
                if isinstance(n, int) and n == -1:
                    dve.wait_ge(whi, 2)
                    dve.tensor_tensor(down[:, 1, :], down_stage, down[:, 0, :], ALU.subtract).then_inc(wsplit, 1)
                    dve.tensor_tensor(wgu[:, 1, :], gu_stage, wgu[:, 0, :], ALU.subtract).then_inc(wsplit, 1)
                for t in range(TPB):
                    if cur and t < TPB - 1:
                        one_hot(n, t + 1, odd)
                    if t == 0 and cur and not (isinstance(n, int) and n == base):
                        residual(n - 1, base)
                    if t == 0 and second and not is_lead(n, base):
                        statistics(n + 2, base)
                    if isinstance(n, int) and n == -1 and t == TPB - 1:
                        dve.wait_ge(pconst, N_CONST)
                    if t == TPB - 1 and nxt:
                        select(n + 1)
                    if nxt and t == TPB - 2:
                        search(n + 1, t + 1)
                    if cur:
                        weigh(n, t)
                    if is_final(n, base) and t != TPB - 2:
                        if t == 1:
                            dve.wait_ge(xt_d, NB)
                        mixing_step(mixing, {0: -3, 1: -2, TPB - 1: -1}[t])
                    if nxt and t < TPB - 2:
                        search(n + 1, t + 1)
                if second:
                    search(n + 2, 0)
                if nxt:
                    spread(n + 1, 1 - odd)
                    one_hot(n + 1, 0, 1 - odd)
                if isinstance(n, int) and n == base + NB - 1:
                    residual(n, base)

            statistics(0, 0)
            dve.wait_ge(key_hi, 2)
            for s in range(2):
                hi, lo = [keyw[:, i, :].rearrange("p (s h2 h1 k) -> p s h2 h1 k", s=2, h2=2, h1=2)[:, s] for i in range(2)]
                dve.tensor_tensor(lo, key_ps[s], hi, ALU.subtract).then_inc(key_split, 1)
            schedule(dve, 0, body)

            def after_last_sums():
                dve.wait_ge(mix_d, NB - 3)
                statistics(NB, NB)

            attention(dve, mixing, {NB - 1: after_last_sums})
            dve.wait_ge(mix_d, NB)
            schedule(dve, 1, body)


def build_args(nc, arrays):
    names = ["x", "w_qkv_t", "w_swiglu_t", "w_out_t", "w_queries", "keys_t", "down_t", "up", "w_gu_t", "w_down_t"]
    return [nc.dram_tensor(n, arrays[n].shape, mybir.dt.from_np(arrays[n].dtype), kind="ExternalInput").ap() for n in names]


def kernel(L0_attn_x, L0_attn_w_qkv, L0_attn_w_swiglu, L0_attn_w_out, L0_ffn_w_queries, L0_ffn_keys,
           L0_ffn_down_embed, L0_ffn_up_embed, L0_ffn_w_gate, L0_ffn_w_up, L0_ffn_w_down):
    import numpy as np
    import concourse.bacc as bacc
    from concourse.bass_utils import run_bass_kernel_spmd

    c = np.ascontiguousarray
    arrays = {
        "x": c(np.asarray(L0_attn_x).reshape(-1, P)),
        "w_qkv_t": c(np.asarray(L0_attn_w_qkv).T),
        "w_swiglu_t": c(np.asarray(L0_attn_w_swiglu).T),
        "w_out_t": c(np.asarray(L0_attn_w_out).T),
        "w_queries": c(np.asarray(L0_ffn_w_queries)),
        "keys_t": c(np.asarray(L0_ffn_keys).transpose(2, 0, 3, 1).reshape(2, H * 32, NK)),
        "down_t": c(np.asarray(L0_ffn_down_embed).T),
        "up": c(np.asarray(L0_ffn_up_embed)),
        "w_gu_t": c(np.concatenate([np.asarray(L0_ffn_w_gate), np.asarray(L0_ffn_w_up)]).T),
        "w_down_t": c(np.asarray(L0_ffn_w_down).T),
    }
    nc = bacc.Bacc("TRN2", target_bir_lowering=False, num_devices=1)
    args = build_args(nc, arrays)
    out = nc.dram_tensor("out", arrays["x"].shape, F32, kind="ExternalOutput").ap()
    emit(nc, *args, out)
    r = run_bass_kernel_spmd(nc, [arrays], core_ids=[0])
    return r.results[0]["out"].reshape(np.asarray(L0_attn_x).shape)
```
